# Optimizing a Trainium2 kernel written in Bass

```python
import numpy as np
import jax
import jax.numpy as jnp

def _softmax(x, axis=-1):
    return jax.nn.softmax(x, axis=axis)

def _gelu(x):
    return jax.nn.gelu(x, approximate=True)

def _silu(x):
    return jax.nn.silu(x)

def _sigmoid(x):
    return jax.nn.sigmoid(x)

def _layernorm(x, axis=-1, eps=1e-05):
    m = jnp.mean(x, axis=axis, keepdims=True)
    v = jnp.var(x, axis=axis, keepdims=True)
    return (x - m) / jnp.sqrt(v + eps)

def _scatter_add(tgt, idx, src, axis=0):
    return tgt.at[idx].add(src)

def _segment_sum(src, seg, n):
    return jax.ops.segment_sum(src, seg, n)
kernel_name = 'mk_gnn_ffn_d1_gnn_r8_44c1ef'

def setup_inputs(seed: int=0):
    np.random.seed(seed)
    _w = jnp.asarray

    def _rec_inputs():
        import jax
        import jax.numpy as jnp
        _gk = jax.random.key(seed)
        x = -0.0003713 + 1 * jax.random.normal(jax.random.fold_in(_gk, 1), (6250, 256), jnp.float32)
        src = jax.random.randint(jax.random.fold_in(_gk, 2), (100000,), 0, 6250, jnp.int32)
        dst = jax.random.randint(jax.random.fold_in(_gk, 3), (100000,), 0, 6250, jnp.int32)
        _o = jnp.argsort(dst, stable=True)
        src = src[_o]
        dst = dst[_o]
        edge_attr_64 = -9.77346e-05 + 0.999888 * jax.random.normal(jax.random.fold_in(_gk, 12), (100000, 64), jnp.float32)
        return (x, src, dst, edge_attr_64)
    x, src, dst, edge_attr_64 = _rec_inputs()

    def _L0_gnn_setup():
        import jax, jax.numpy as jnp
        import numpy as np
        ALPHA = 0.2
        key = jax.random.key(seed)
        ks = jax.random.split(key, 6)
        N, E, F_IN, F_OUT, E_DIM = (6250, 100000, 256, 256, 64)
        h = jax.random.normal(ks[0], (N, F_IN), dtype=jnp.float32)
        e_feat = jax.random.normal(ks[1], (E, E_DIM), dtype=jnp.float32)
        W = jax.random.normal(ks[2], (F_OUT, F_IN), dtype=jnp.float32) * (1.0 / np.sqrt(F_IN))
        A = jax.random.normal(ks[3], (1, 2 * F_OUT + E_DIM), dtype=jnp.float32) * 0.05
        src = jax.random.randint(ks[4], (E,), 0, N, dtype=jnp.int32)
        dst = jax.random.randint(ks[5], (E,), 0, N, dtype=jnp.int32)
        return {'h': h, 'e_feat': e_feat, 'W': W, 'A': A, 'src': src, 'dst': dst}
    _L0_gnn_all = _L0_gnn_setup()
    _L0_gnn_in = {k: v for k, v in _L0_gnn_all.items() if k in ('W', 'A')}
    del _L0_gnn_all

    def _L0_ffn_setup():
        import jax, jax.numpy as jnp
        import numpy as np
        BN_EPS = 0.001

        def _bn(h, g, b, m, v):
            return g * (h - m) * jax.lax.rsqrt(v + BN_EPS) + b
        key = jax.random.key(seed)
        ks = jax.random.split(key, 8)
        B, F, Df = (256, 64, 256)
        E, H, D = (8, 256, 256)
        s1 = 1.0 / np.sqrt(Df)
        s2 = 1.0 / np.sqrt(H)
        return {'x': jax.random.normal(ks[0], (B, F, Df), jnp.float32), 'Wr': jax.random.normal(ks[1], (Df, E), jnp.float32) * s1, 'br': jnp.zeros((E,), jnp.float32), 'W1': jax.random.normal(ks[2], (E, Df, H), jnp.float32) * s1, 'b1': jnp.zeros((E, H), jnp.float32), 'g1': jnp.ones((E, H), jnp.float32), 'be1': jnp.zeros((E, H), jnp.float32), 'm1': jnp.zeros((E, H), jnp.float32), 'v1': jnp.ones((E, H), jnp.float32), 'W2': jax.random.normal(ks[3], (E, H, H), jnp.float32) * s2, 'b2': jnp.zeros((E, H), jnp.float32), 'g2': jnp.ones((E, H), jnp.float32), 'be2': jnp.zeros((E, H), jnp.float32), 'm2': jnp.zeros((E, H), jnp.float32), 'v2': jnp.ones((E, H), jnp.float32), 'Wo': jax.random.normal(ks[4], (E, H, D), jnp.float32) * s2, 'bo': jnp.zeros((E, D), jnp.float32)}
    _L0_ffn_all = _L0_ffn_setup()
    _L0_ffn_in = {k: v for k, v in _L0_ffn_all.items() if k in ('Wr', 'br', 'W1', 'b1', 'g1', 'be1', 'm1', 'v1', 'W2', 'b2', 'g2', 'be2', 'm2', 'v2', 'Wo', 'bo')}
    del _L0_ffn_all
    return {'x': x, 'src': src, 'dst': dst, 'edge_attr_64': edge_attr_64, 'L0_gnn_W': _L0_gnn_in['W'], 'L0_gnn_A': _L0_gnn_in['A'], 'L0_ffn_Wr': _L0_ffn_in['Wr'], 'L0_ffn_br': _L0_ffn_in['br'], 'L0_ffn_W1': _L0_ffn_in['W1'], 'L0_ffn_b1': _L0_ffn_in['b1'], 'L0_ffn_g1': _L0_ffn_in['g1'], 'L0_ffn_be1': _L0_ffn_in['be1'], 'L0_ffn_m1': _L0_ffn_in['m1'], 'L0_ffn_v1': _L0_ffn_in['v1'], 'L0_ffn_W2': _L0_ffn_in['W2'], 'L0_ffn_b2': _L0_ffn_in['b2'], 'L0_ffn_g2': _L0_ffn_in['g2'], 'L0_ffn_be2': _L0_ffn_in['be2'], 'L0_ffn_m2': _L0_ffn_in['m2'], 'L0_ffn_v2': _L0_ffn_in['v2'], 'L0_ffn_Wo': _L0_ffn_in['Wo'], 'L0_ffn_bo': _L0_ffn_in['bo']}

def reference(x, src, dst, edge_attr_64, L0_gnn_W, L0_gnn_A, L0_ffn_Wr, L0_ffn_br, L0_ffn_W1, L0_ffn_b1, L0_ffn_g1, L0_ffn_be1, L0_ffn_m1, L0_ffn_v1, L0_ffn_W2, L0_ffn_b2, L0_ffn_g2, L0_ffn_be2, L0_ffn_m2, L0_ffn_v2, L0_ffn_Wo, L0_ffn_bo):
    import jax
    import jax.numpy as jnp

    def _L0_gnn_ref(h, e_feat, W, A, src, dst):
        import jax, jax.numpy as jnp
        import numpy as np
        ALPHA = 0.2
        N = h.shape[0]
        F_OUT = W.shape[0]
        z = h @ W.T
        z_src = z[src]
        z_dst = z[dst]
        a_src, a_dst, a_e = (A[0, :F_OUT], A[0, F_OUT:2 * F_OUT], A[0, 2 * F_OUT:])
        logits = z_src @ a_src + z_dst @ a_dst + e_feat @ a_e
        e = jax.nn.leaky_relu(logits, ALPHA)
        m = jax.ops.segment_max(e, dst, num_segments=N)
        ex = jnp.exp(e - m[dst])
        denom = jax.ops.segment_sum(ex, dst, num_segments=N)
        alpha = ex / denom[dst]
        h_out = jax.ops.segment_sum(alpha[:, None] * z_src, dst, num_segments=N)
        return h_out

    def _L0_ffn_ref(x, Wr, br, W1, b1, g1, be1, m1, v1, W2, b2, g2, be2, m2, v2, Wo, bo):
        import jax, jax.numpy as jnp
        import numpy as np
        BN_EPS = 0.001

        def _bn(h, g, b, m, v):
            return g * (h - m) * jax.lax.rsqrt(v + BN_EPS) + b
        feat = jnp.mean(x, axis=0)
        w = jax.nn.softmax(feat @ Wr + br, axis=-1)
        h = jnp.einsum('bfd,edh->bfeh', x, W1) + b1
        h = jax.nn.relu(_bn(h, g1, be1, m1, v1))
        h = jnp.einsum('bfeh,ehk->bfek', h, W2) + b2
        h = jax.nn.relu(_bn(h, g2, be2, m2, v2))
        y = jnp.einsum('bfeh,ehd->bfed', h, Wo) + bo
        return jnp.einsum('bfed,fe->bfd', y, w)
    x = x + _L0_gnn_ref(_layernorm(x, axis=-1), edge_attr_64, L0_gnn_W, L0_gnn_A, src, dst)
    x = x + _L0_ffn_ref(_layernorm(x, axis=-1)[None], L0_ffn_Wr, L0_ffn_br, L0_ffn_W1, L0_ffn_b1, L0_ffn_g1, L0_ffn_be1, L0_ffn_m1, L0_ffn_v1, L0_ffn_W2, L0_ffn_b2, L0_ffn_g2, L0_ffn_be2, L0_ffn_m2, L0_ffn_v2, L0_ffn_Wo, L0_ffn_bo)[0]
    return x

_drawn_inputs = setup_inputs


def setup_inputs(seed=0):
    import zlib

    import numpy as np

    out = dict(_drawn_inputs(seed))
    spreads = {'L0_ffn_br': (0.0, 0.1),
     'L0_ffn_b1': (0.0, 0.335),
     'L0_ffn_g1': (1.0, 0.2),
     'L0_ffn_be1': (0.0, 0.341),
     'L0_ffn_m1': (0.0, 0.332),
     'L0_ffn_v1': (1.0, 0.6),
     'L0_ffn_b2': (0.0, 0.1),
     'L0_ffn_g2': (1.0, 0.2),
     'L0_ffn_be2': (0.0, 0.1),
     'L0_ffn_m2': (0.0, 0.1),
     'L0_ffn_v2': (1.0, 0.582),
     'L0_ffn_bo': (0.0, 0.1)}
    factors = {}
    for name, (base, spread) in spreads.items():
        noise = np.random.default_rng([zlib.crc32(name.encode()), seed]).standard_normal(out[name].shape)
        drawn = base * np.exp(spread * noise) if base else spread * noise
        out[name] = jnp.asarray(drawn.astype(out[name].dtype))
    for name, factor in factors.items():
        out[name] = (out[name] * factor).astype(out[name].dtype)
    return out
```

```python
from contextlib import ExitStack

import concourse.bass as bass
from concourse import mybir

F32 = mybir.dt.float32
BF16 = mybir.dt.bfloat16
I32 = mybir.dt.int32
U32 = mybir.dt.uint32
ALU = mybir.AluOpType
ACT = mybir.ActivationFunctionType
AX = mybir.AxisListType

NODES, EDGES, F, EDIM, EXPERTS = 6250, 100000, 256, 64, 8
NB = 125
BLOCKS = NODES // NB
GROUPS = BLOCKS // 2
TILES = 17
CAP = TILES * 128
ROW = F + 2
KC = F // 128
SPAN = 32
ROWS_D = EDGES // SPAN
PS = 125
CB = 5
CHUNKS = BLOCKS // CB
ALPHA, LN_EPS, BN_EPS = 0.2, 1e-5, 1e-3
FAR = 1e30
NT_ROUNDS = [(0, 6), (6, 12), (12, 17)]

STEPS = {
    0: [("edges", 0)],
    1: [("nt0", 0)],
    2: [("scores", 0), ("nt1", 0)],
    3: [("nt2", 0), ("colmax", 0)],
    4: [("nodemax", 0)],
    5: [("spread", 0), ("edges", 1)],
    6: [("weights", 0), ("nt0", 1)],
    7: [("scores", 1), ("nt1", 1)],
    8: [("aggregate", 0), ("nt2", 1), ("colmax", 1)],
    9: [("nodemax", 1), ("turn", 0)],
    10: [("spread", 1), ("project", 0)],
    11: [("weights", 1)],
    13: [("aggregate", 1)],
    14: [("turn", 1)],
    15: [("project", 1)],
    16: [("moments", None)],
    17: [("normalise", None)],
    19: [("turn_x", None)],
    20: [("route", None)],
    21: [("gates", None)],
    22: [("turn_w", None)],
    23: [("base", None)],
}
SLOTS = 24


def layer_order():
    out = []
    for n in range(EXPERTS + 2):
        for layer, e in ((1, n), (2, n - 1), (3, n - 2)):
            if 0 <= e < EXPERTS:
                out.append((layer, e))
    return out


LAYERS = layer_order()


def gnn_ffn_program(nc, x, src, dst, edge_attr, gnn_W, gnn_A, Wr, br, W1, b1, g1, be1, m1, v1,
                    W2, b2, g2, be2, m2, v2, Wo, bo, out):
    table = nc.dram_tensor("table", (NODES, ROW), F32, kind="Internal").ap()
    dst_rows = dst.rearrange("(r s) -> r s", s=SPAN)
    x_blocks = x.rearrange("(b p) f -> p b f", p=NB)
    table_blocks = table.rearrange("(b p) f -> p b f", p=NB)

    with ExitStack() as ctx:
        def sb(name, shape, dt=F32):
            return ctx.enter_context(nc.sbuf_tensor(name, shape, dt))

        def sem(name):
            return ctx.enter_context(nc.semaphore(name))

        def pair(name):
            return [sem(f"{name}{q}") for q in range(2)]

        def bank(name, dt=F32):
            return ctx.enter_context(nc.psum_tensor(name, [128, 2048 // (2 if dt == BF16 else 4)], dt))

        w1 = sb("w1", [128, EXPERTS * KC, F])
        w2 = sb("w2", [128, EXPERTS * KC, F])
        wo = sb("wo", [128, EXPERTS * KC, F])
        gw = sb("gw", [128, KC, F])
        gwT = sb("gwT", [128, KC, F])
        a_cols = sb("a_cols", [128, 2 * KC])
        a_wide = sb("a_wide", [128, 2 * KC, 128])
        a_e = sb("a_e", [128, EDIM])
        u_rows = sb("u_rows", [128, 2, F])
        wr = sb("wr", [128, KC, EXPERTS])
        br_row = sb("br_row", [1, EXPERTS])
        bo_sb = sb("bo_sb", [EXPERTS, F])
        bn_in = sb("bn_in", [EXPERTS * KC, 10, 128])
        bn_tmp = sb("bn_tmp", [EXPERTS * KC, 2, 128])
        bn_rows = sb("bn_rows", [EXPERTS * KC, 4, 128])
        bn_cols = sb("bn_cols", [128, 4, EXPERTS * KC])
        ident = sb("ident", [128, 128])
        ident_b = sb("ident_b", [128, 128], BF16)
        ones = sb("ones", [128, 128])
        eps_ln = sb("eps_ln", [128, 1])
        eps_bn = sb("eps_bn", [128, 1])
        dst_all = sb("dst_all", [PS, EDGES // PS], I32)
        bound_row_i = sb("bound_row_i", [128, BLOCKS], I32)
        bound_row = sb("bound_row", [128, BLOCKS])
        bound_col_i = sb("bound_col_i", [BLOCKS, 1], I32)
        bound_col = sb("bound_col", [BLOCKS, 1])
        below = sb("below", [PS, BLOCKS, EDGES // PS // SPAN])
        below_n = sb("below_n", [PS, BLOCKS])
        row_f = sb("row_f", [BLOCKS, 1])
        row_i = sb("row_i", [BLOCKS, 1], I32)
        window = sb("window", [BLOCKS, SPAN], I32)
        in_row = sb("in_row", [BLOCKS, SPAN])
        in_row_n = sb("in_row_n", [BLOCKS, 1])
        start_col = sb("start_col", [BLOCKS, 1])
        starts = sb("starts", [1, BLOCKS], I32)
        st6 = sb("st6", [NB, 2, CB, 6])
        mv = sb("mv", [NB, 2, CB, 2])
        std = sb("std", [NB, 2, CB])
        rstd = sb("rstd", [NB, 2, CB])
        nmr = sb("nmr", [NB, 2, CB])
        dots = sb("dots", [NB, 2, 2, CB])
        junk = sb("junk", [NB, 2, F])
        sdst = sb("sdst", [NB, BLOCKS])
        sdst_r = sb("sdst_r", [NB, BLOCKS])
        sdst3 = sb("sdst3", [NB, BLOCKS, 3], BF16)
        ids_i = sb("ids_i", [128, 2 * NB], I32)
        ids = sb("ids", [128, 2, NB])
        two_blocks = sb("two_blocks", [128, NB])
        src_t = sb("src_t", [128, 2, TILES], I32)
        dst_t = sb("dst_t", [128, 2, TILES], I32)
        attr = sb("attr", [128, 2, TILES, EDIM])
        x_in = sb("x_in", [NB, 2, F])
        rows = sb("rows", [128, 2, TILES, ROW])
        early = rows.rearrange("p q j f -> p (q j f)")
        XC, TR = 2 * CB * F, 2 * CB * ROW
        xc = early[0:NB, 0:XC].rearrange("p (q b f) -> p q b f", q=2, b=CB)
        tr = early[0:NB, XC:XC + TR].rearrange("p (q b f) -> p q b f", q=2, b=CB)
        prod = sb("prod", [128, TILES, EDIM])
        s_edge = sb("s_edge", [128, TILES])
        t_edge = sb("t_edge", [128, 2, TILES])
        other = sb("other", [128, 2, TILES, NB], BF16)
        masked = sb("masked", [128, TILES, NB])
        colmax = sb("colmax", [128, NB])
        mine_T = sb("mine_T", [NB, TILES, 128], BF16)
        node_t = sb("node_t", [NB, 4])
        node6 = sb("node6", [NB, 6], BF16)
        spread = sb("spread", [128, TILES, 2])
        logit = sb("logit", [128, TILES])
        score = sb("score", [128, TILES])
        ex = sb("ex", [128, TILES])
        wgt = sb("wgt", [128, TILES, NB])
        den = sb("den", [NB, 2])
        agg = sb("agg", [NB, F])
        aggT = sb("aggT", [128, KC, NB])
        x1 = sb("x1", [NB, 2, F])
        ln6 = sb("ln6", [NB, 2, 6])
        lnmv = sb("lnmv", [NB, 2, 2])
        lnstd = sb("lnstd", [NB, 2])
        lnr = sb("lnr", [NB, 2])
        xn = sb("xn", [NB, 2, F])
        xT = sb("xT", [128, KC, 2 * NB])
        r_negmax = sb("r_negmax", [NB, 2])
        r_exp = sb("r_exp", [NB, 2, EXPERTS])
        r_sum = sb("r_sum", [NB, 2])
        r_inv = sb("r_inv", [NB, 2])
        r_w = sb("r_w", [NB, 2, EXPERTS])
        r_wT = sb("r_wT", [EXPERTS, 2 * NB])
        gate = sb("gate", [NB, 2, EXPERTS])
        base = sb("base", [NB, 2, F])
        h1 = sb("h1", [128, 2, KC, 2 * NB])
        h2 = sb("h2", [128, 2, KC, 2 * NB])
        acc = sb("acc", [NB, 2, F])

        p_agg = bank("p_agg")
        p_nt = [bank("p_nt0", BF16), bank("p_nt1", BF16)]
        p_att = bank("p_att")
        p_mix = bank("p_mix")
        p_l1 = bank("p_l1")
        p_l2 = bank("p_l2")
        p_l3 = bank("p_l3")

        l_gnn = sem("l_gnn")
        l_dst = sem("l_dst")
        l_bn = sem("l_bn")
        l_small = sem("l_small")
        l_w = sem("l_w")
        l_x = pair("l_x")
        consts_ready = sem("consts_ready")
        gwT_done = sem("gwT_done")
        awide_ready = sem("awide_ready")
        u_done = sem("u_done")
        gw_copied = sem("gw_copied")
        counts_ready = sem("counts_ready")
        counts_summed = sem("counts_summed")
        row_ready = sem("row_ready")
        window_loaded = sem("window_loaded")
        start_ready = sem("start_ready")
        start_turned = sem("start_turned")
        starts_ready = sem("starts_ready")
        bn_var_ready = sem("bn_var_ready")
        bn_rows_ready = sem("bn_rows_ready")
        bn_turned = sem("bn_turned")
        bn_cols_ready = sem("bn_cols_ready")
        stats_ready = sem("stats_ready")
        std_ready = sem("std_ready")
        rstd_ready = sem("rstd_ready")
        table_rows = sem("table_rows")
        table_dots = sem("table_dots")
        table_stored = pair("table_stored")
        edges_loaded = pair("edges_loaded")
        x_loaded = pair("x_loaded")
        ids_ready = pair("ids_ready")
        gathered = pair("gathered")
        other_ready = pair("other_ready")
        nt_done = sem("nt_done")
        mine_ready = sem("mine_ready")
        colmax_ready = sem("colmax_ready")
        colmax_turned = sem("colmax_turned")
        node_ready = sem("node_ready")
        spread_done = sem("spread_done")
        score_ready = sem("score_ready")
        exp_ready = sem("exp_ready")
        wgt_ready = sem("wgt_ready")
        agg_done = sem("agg_done")
        agg_ready = sem("agg_ready")
        agg_turned = sem("agg_turned")
        aggT_ready = sem("aggT_ready")
        projected = sem("projected")
        x1_ready = sem("x1_ready")
        moments_ready = sem("moments_ready")
        lnstd_ready = sem("lnstd_ready")
        xn_ready = sem("xn_ready")
        x_turned = sem("x_turned")
        xT_ready = sem("xT_ready")
        routed = sem("routed")
        negmax_ready = sem("negmax_ready")
        r_exp_ready = sem("r_exp_ready")
        r_w_ready = sem("r_w_ready")
        w_turned = sem("w_turned")
        wT_ready = sem("wT_ready")
        bias_done = sem("bias_done")
        base_ready = sem("base_ready")
        l1_done = sem("l1_done")
        h1_ready = sem("h1_ready")
        l2_done = sem("l2_done")
        h2_ready = sem("h2_ready")
        l3_done = sem("l3_done")
        y_added = sem("y_added")
        out_stored = sem("out_stored")

        def wait(eng, semaphore, value):
            if not isinstance(value, int) or value > 0:
                eng.wait_ge(semaphore, value)

        def over_groups(eng, attention, experts, slots=True):
            def group(i, attend, expert):
                for s in range(SLOTS):
                    if expert:
                        experts(i - 1, *LAYERS[s])
                    if attend:
                        for what, q in STEPS.get(s, []):
                            attention(i, what, q)
            group(0, True, False)
            with eng.Fori(1, GROUPS) as i:
                group(i, True, True)
            group(GROUPS, False, True)

        block = ctx.enter_context(nc.Block())

        @block.sync
        def _(sp):
            sp.dma_start(gw[:], gnn_W.rearrange("(c p) f -> p c f", p=128)).then_inc(l_gnn, 16)
            sp.dma_start(a_cols[:], gnn_A[0, 0:2 * F].rearrange("(c p) -> p c", p=128), allow_slow_non_contiguous=True).then_inc(l_gnn, 16)
            sp.dma_start(a_e[:], gnn_A[0:1, 2 * F:2 * F + EDIM].broadcast_to([128, EDIM])).then_inc(l_gnn, 16)
            sp.dma_start(xc[:, 0], x_blocks[:, 0:CB, :]).then_inc(l_x[0], 16)
            sp.dma_start(dst_all[:], dst.rearrange("(p n) -> p n", p=PS)).then_inc(l_dst, 16)
            sp.dma_start(xc[:, 1], x_blocks[:, CB:2 * CB, :]).then_inc(l_x[1], 16)
            for n, a in enumerate((b1, g1, be1, m1, v1, b2, g2, be2, m2, v2)):
                sp.dma_start(bn_in[:, n, :], a.rearrange("e (c p) -> (e c) p", p=128)).then_inc(l_bn, 16)
            sp.dma_start(wr[:], Wr.rearrange("(c p) e -> p c e", p=128)).then_inc(l_small, 16)
            sp.dma_start(br_row[:], br.rearrange("(o e) -> o e", o=1)).then_inc(l_small, 16)
            sp.dma_start(bo_sb[:], bo).then_inc(l_small, 16)

            def store_rows(c, q, last=False):
                sp.wait_ge(table_dots, c + 1)
                sp.dma_start(table_blocks[:, bass.ds(c * CB, CB), :], tr[:, q]).then_inc(table_stored[q], 16)
                if not last:
                    sp.dma_start(xc[:, q], x_blocks[:, bass.ds(c * CB + 2 * CB, CB), :]).then_inc(l_x[q], 16)

            with sp.Fori(0, CHUNKS // 2 - 1) as i:
                for q in range(2):
                    store_rows(i * 2 + q, q)
            for q in range(2):
                store_rows(CHUNKS - 2 + q, q, last=True)
            sp.wait_ge(starts_ready, 1)

            def load_edges(i, q):
                first = sp.value_load(starts[0:1, bass.ds(i * 2 + q, 1)], min_val=0, max_val=EDGES - CAP)
                for t, of in ((src_t, src), (dst_t, dst)):
                    sp.dma_start(t[:, q, :], of[bass.ds(first, CAP)].rearrange("(p j) -> p j", j=TILES)).then_inc(edges_loaded[q], 16)
                sp.dma_start(attr[:, q], edge_attr[bass.ds(first, CAP), :].rearrange("(p j) d -> p j d", j=TILES)).then_inc(edges_loaded[q], 16)

            def load_x(i, q):
                sp.dma_start(x_in[:, q, :], x[bass.ds(i * (2 * NB) + q * NB, NB), :]).then_inc(x_loaded[q], 16)

            def store_out(g):
                sp.wait_ge(y_added, g * EXPERTS + EXPERTS + 1)
                sp.dma_start(out[bass.ds(g * (2 * NB), 2 * NB), :].rearrange("(q p) f -> p q f", p=NB), acc[:]).then_inc(out_stored, 16)

            def next_loads(i):
                for q in range(2):
                    sp.wait_ge(gathered[q], i * (16 * TILES))
                    sp.wait_ge(other_ready[q], i)
                    load_edges(i, q)
                for q in range(2):
                    sp.wait_ge(x1_ready, i * 2 - 1 + q)
                    load_x(i, q)

            for q in range(2):
                load_edges(0, q)
                load_x(0, q)
            for t, w in ((w1, W1), (w2, W2), (wo, Wo)):
                sp.dma_start(t[:], w.rearrange("e (c p) f -> p (e c) f", p=128)).then_inc(l_w, 16)
            next_loads(1)
            with sp.Fori(2, GROUPS) as i:
                next_loads(i)
                store_out(i - 2)
            store_out(GROUPS - 2)
            store_out(GROUPS - 1)
            sp.wait_ge(out_stored, 16 * (GROUPS + 1))

        @block.gpsimd
        def _(pool):
            nc.gpsimd.memset(ones[:], 1.0)
            nc.gpsimd.memset(ident[:], 0.0)
            nc.gpsimd.memset(eps_ln[:], LN_EPS)
            nc.gpsimd.memset(eps_bn[:], BN_EPS)
            nc.gpsimd.memset(two_blocks[:], float(2 * NB))
            nc.gpsimd.iota(bound_row_i[:], pattern=[[NB, BLOCKS]], base=0, channel_multiplier=0)
            nc.gpsimd.iota(bound_col_i[:], pattern=[[0, 1]], base=0, channel_multiplier=NB)
            nc.gpsimd.iota(ids_i[:], pattern=[[1, 2 * NB]], base=0, channel_multiplier=0)
            pool.drain()
            nc.gpsimd.affine_select(out=ident[:], in_=ident[:], compare_op=ALU.not_equal, fill=1.0, base=0,
                                    pattern=[[-1, 128]], channel_multiplier=1)
            nc.gpsimd.tensor_copy(bound_row[:], bound_row_i[:])
            nc.gpsimd.tensor_copy(bound_col[:], bound_col_i[:])
            nc.gpsimd.tensor_scalar(ids.rearrange("p q n -> p (q n)"), ids_i[:], float(-2 * NB), None, ALU.add)
            pool.drain()
            nc.gpsimd.tensor_copy(ident_b[:], ident[:]).then_inc(consts_ready, 1)
            pool.wait_ge(row_ready, 1)
            nc.gpsimd.indirect_dma_start(window[:], None, dst_rows, bass.IndirectOffsetOnAxis(ap=row_i[:].bitcast(U32), axis=0)).then_inc(window_loaded, 16)
            for q in range(2):
                pool.wait_ge(table_stored[q], 16 * (CHUNKS // 2))

            def gather(i, q):
                wait(pool, other_ready[q], i)
                wait(pool, agg_done, i * 2 + q - 1)
                pool.wait_ge(edges_loaded[q], i * 48 + 48)
                nc.gpsimd.tensor_tensor(ids[:, q, :], ids[:, q, :], two_blocks[:], ALU.add).then_inc(ids_ready[q], 1)
                for j in range(TILES):
                    nc.gpsimd.indirect_dma_start(
                        rows[:, q, j, :], None, table,
                        bass.IndirectOffsetOnAxis(ap=src_t[:, q, j:j + 1].bitcast(U32), axis=0)).then_inc(gathered[q], 16)

            for q in range(2):
                gather(0, q)
            with pool.Fori(1, GROUPS) as i:
                for q in range(2):
                    gather(i, q)

        @block.scalar
        def _(act):
            act.nop().then_inc(h1_ready, 1)
            act.nop().then_inc(h2_ready, 1)
            act.nop().then_inc(out_stored, 16)
            act.wait_ge(consts_ready, 1)
            act.wait_ge(l_bn, 160)
            for l in range(2):
                last = nc.scalar.activation(bn_tmp[:, l, :], bn_in[:, 5 * l + 4, :], ACT.Sqrt, bias=eps_bn[0:EXPERTS * KC, :])
            last.then_inc(bn_var_ready, 1)

            def table_chunk(c, q):
                act.wait_ge(stats_ready, c + 1)
                nc.scalar.activation(std[:, q, :], mv[:, q, :, 1], ACT.Sqrt, bias=eps_ln[0:NB, :]).then_inc(std_ready, 1)
                act.wait_ge(rstd_ready, c + 1)
                wait(act, table_stored[q], (c - q) * 8)
                for b in range(CB):
                    last = nc.scalar.activation(tr[:, q, b, 0:F], xc[:, q, b, :], ACT.Identity,
                                                bias=nmr[:, q, b:b + 1], scale=rstd[:, q, b:b + 1])
                last.then_inc(table_rows, 1)

            for q in range(2):
                table_chunk(q, q)
            with act.Fori(1, CHUNKS // 2) as i:
                for q in range(2):
                    table_chunk(i * 2 + q, q)

            def attention(i, what, q):
                b = i * 2 + (q or 0)
                if what in ("nt0", "nt1", "nt2"):
                    r = int(what[2])
                    lo, hi = NT_ROUNDS[r]
                    act.wait_ge(nt_done, b * 3 + r + 1)
                    if r == 0:
                        wait(act, spread_done, b)
                    nc.scalar.activation(mine_T[:, lo:hi, :].rearrange("p j e -> p (j e)"),
                                         p_nt[(r) % 2][0:NB, 0:(hi - lo) * 128], ACT.Copy, bias=1.0, scale=-1.0).then_inc(mine_ready, 1)
                elif what == "weights":
                    act.wait_ge(score_ready, b + 1)
                    wait(act, wgt_ready, b)
                    nc.scalar.activation(ex[:], score[:], ACT.Exp).then_inc(exp_ready, 1)
                elif what == "turn":
                    act.wait_ge(agg_turned, b + 1)
                    nc.scalar.activation(aggT.rearrange("p c n -> p (c n)"), p_mix[:, 0:KC * NB], ACT.Copy).then_inc(aggT_ready, 1)
                elif what == "moments":
                    act.wait_ge(moments_ready, i + 1)
                    nc.scalar.activation(lnstd[:], lnmv[:, :, 1], ACT.Sqrt, bias=eps_ln[0:NB, :]).then_inc(lnstd_ready, 1)
                elif what == "turn_x":
                    act.wait_ge(x_turned, i + 1)
                    nc.scalar.activation(xT.rearrange("p c n -> p (c n)"), p_mix[:, 0:KC * 2 * NB], ACT.Copy).then_inc(xT_ready, 1)
                elif what == "route":
                    act.wait_ge(negmax_ready, i + 1)
                    for z in range(2):
                        last = nc.scalar.activation(r_exp[:, z, :], p_mix[0:NB, z * EXPERTS:(z + 1) * EXPERTS], ACT.Exp,
                                                    bias=r_negmax[:, z:z + 1], accum_out=r_sum[:, z:z + 1])
                    last.then_inc(r_exp_ready, 1)
                elif what == "turn_w":
                    act.wait_ge(w_turned, i + 1)
                    nc.scalar.activation(r_wT[:], p_mix[0:EXPERTS, 0:2 * NB], ACT.Copy).then_inc(wT_ready, 1)

            def experts(g, layer, e):
                n = g * EXPERTS + e
                if layer == 3:
                    return
                done, bank_, h, ready = ((l1_done, p_l1, h1, h1_ready), (l2_done, p_l2, h2, h2_ready))[layer - 1]
                act.wait_ge(done, n + 1)
                if False:
                    act.wait_ge(bn_cols_ready, 1)
                for m in range(KC):
                    k = e * KC + m
                    last = nc.scalar.activation(h[:, e % 2, m, :], bank_[:, m * 2 * NB:(m + 1) * 2 * NB], ACT.Relu,
                                                bias=bn_cols[:, 2 * layer - 1, k:k + 1], scale=bn_cols[:, 2 * layer - 2, k:k + 1])
                last.then_inc(ready, 1)

            act.wait_ge(bn_cols_ready, 1)
            over_groups(act, attention, experts)

        @block.vector
        def _(v):
            V = nc.vector
            v.nop().then_inc(y_added, 1)
            V.memset(tr[:, :, :, F:F + 1], 1.0)
            v.wait_ge(l_gnn, 48)
            V.tensor_copy(a_wide[:], a_cols[:].unsqueeze(2).broadcast_to([128, 2 * KC, 128])).then_inc(awide_ready, 1)

            def stats(c, q):
                v.wait_ge(l_x[q], (c - q) * 8 + 16)
                for b in range(CB):
                    V.bn_stats(st6[:, q, b, :], xc[:, q, b, :])
                v.drain()
                for b in range(CB):
                    last = V.bn_aggr(mv[:, q, b, :], st6[:, q, b, :])
                last.then_inc(stats_ready, 1)

            def scale(c, q):
                v.wait_ge(std_ready, c + 1)
                V.reciprocal(rstd[:, q, :], std[:, q, :])
                v.drain()
                V.scalar_tensor_tensor(out=nmr[:, q, :], in0=mv[:, q, :, 0], scalar=-1.0, in1=rstd[:, q, :],
                                       op0=ALU.mult, op1=ALU.mult).then_inc(rstd_ready, 1)

            def dot_rows(c, q):
                v.wait_ge(table_rows, c + 1)
                for b in range(CB):
                    V.tensor_tensor_reduce(junk[:, 0, :], tr[:, q, b, 0:F], u_rows[0:NB, 0, :], 1.0, 0.0, ALU.mult, ALU.add,
                                           dots[:, q, 0, b:b + 1])
                    V.tensor_tensor_reduce(junk[:, 1, :], tr[:, q, b, 0:F], u_rows[0:NB, 1, :], 1.0, 0.0, ALU.mult, ALU.add,
                                           dots[:, q, 1, b:b + 1])
                    v.drain()
                V.tensor_copy(tr[:, q, :, F + 1], dots[:, q, 0, :]).then_inc(table_dots, 1)
                V.tensor_copy(sdst[:, bass.ds(c * CB, CB)], dots[:, q, 1, :])

            stats(0, 0)
            v.wait_ge(l_dst, 16)
            v.wait_ge(consts_ready, 1)
            n_s = EDGES // PS // SPAN
            V.tensor_tensor(below[:], dst_all.rearrange("p (n s) -> p n s", s=SPAN)[:, :, 0].unsqueeze(1).broadcast_to([PS, BLOCKS, n_s]),
                            bound_row[0:PS, :].unsqueeze(2).broadcast_to([PS, BLOCKS, n_s]), ALU.is_lt)
            v.drain()
            V.tensor_reduce(below_n[:], below[:], AX.X, ALU.add).then_inc(counts_ready, 1)
            v.wait_ge(gwT_done, 1)
            V.tensor_copy(gwT.rearrange("p c f -> p (c f)"), p_l1[:, :]).then_inc(gw_copied, 1)
            v.wait_ge(u_done, 1)
            V.tensor_copy(u_rows.rearrange("p s f -> p (s f)"), p_l2[:, :])
            v.wait_ge(counts_summed, 1)
            V.tensor_scalar(row_f[:], p_att[0:BLOCKS, 0:1], -1.0, 0.0, ALU.add, ALU.max)
            v.drain()
            V.tensor_copy(row_i[:], row_f[:]).then_inc(row_ready, 1)
            scale(0, 0)
            stats(1, 1)
            v.wait_ge(window_loaded, 16)
            V.tensor_scalar(in_row[:], window[:], bound_col[:, 0:1], None, ALU.is_lt)
            v.drain()
            V.tensor_reduce(in_row_n[:], in_row[:], AX.X, ALU.add)
            v.drain()
            V.scalar_tensor_tensor(out=start_col[:], in0=row_f[:], scalar=float(SPAN), in1=in_row_n[:], op0=ALU.mult, op1=ALU.add)
            v.drain()
            V.tensor_scalar(start_col[:], start_col[:], float(EDGES - CAP), None, ALU.min).then_inc(start_ready, 1)
            v.wait_ge(bn_var_ready, 1)
            V.reciprocal(bn_tmp[:], bn_tmp[:])
            v.drain()
            for l in range(2):
                V.tensor_tensor(bn_rows[:, 2 * l, :], bn_in[:, 5 * l + 1, :], bn_tmp[:, l, :], ALU.mult)
                V.tensor_tensor(bn_rows[:, 2 * l + 1, :], bn_in[:, 5 * l, :], bn_in[:, 5 * l + 3, :], ALU.subtract)
                v.drain()
                V.tensor_tensor(bn_rows[:, 2 * l + 1, :], bn_rows[:, 2 * l + 1, :], bn_rows[:, 2 * l, :], ALU.mult)
                v.drain()
                last = V.tensor_tensor(bn_rows[:, 2 * l + 1, :], bn_rows[:, 2 * l + 1, :], bn_in[:, 5 * l + 2, :], ALU.add)
            last.then_inc(bn_rows_ready, 1)
            v.wait_ge(start_turned, 1)
            V.tensor_copy(starts[:], p_att[0:1, 64:64 + BLOCKS]).then_inc(starts_ready, 1)
            v.wait_ge(bn_turned, 1)
            V.tensor_copy(bn_cols.rearrange("p n k -> p (n k)"), p_l3[:, 0:4 * EXPERTS * KC]).then_inc(bn_cols_ready, 1)

            dot_rows(0, 0)
            with v.Fori(0, CHUNKS // 2 - 1) as i:
                for q in (1, 0):
                    c = i * 2 + (1 if q else 2)
                    scale(c, q)
                    stats(c + 1, 1 - q)
                    dot_rows(c, q)
            scale(CHUNKS - 1, 1)
            dot_rows(CHUNKS - 1, 1)
            v.drain()
            V.tensor_copy(sdst3[:, :, 0], sdst[:])
            v.drain()
            V.tensor_tensor(sdst_r[:], sdst[:], sdst3[:, :, 0], ALU.subtract)
            v.drain()
            V.tensor_copy(sdst3[:, :, 1], sdst_r[:])
            v.drain()
            V.tensor_tensor(sdst_r[:], sdst_r[:], sdst3[:, :, 1], ALU.subtract)
            v.drain()
            V.tensor_copy(sdst3[:, :, 2], sdst_r[:])

            def attention(i, what, q):
                b = i * 2 + (q or 0)
                if what == "edges":
                    v.drain()
                    v.wait_ge(edges_loaded[q], i * 48 + 48)
                    V.tensor_tensor(prod[:], attr[:, q], a_e[:].unsqueeze(1).broadcast_to([128, TILES, EDIM]), ALU.mult)
                    v.drain()
                    V.tensor_reduce(s_edge[:], prod[:], AX.X, ALU.add)
                    v.wait_ge(ids_ready[q], i + 1)
                    wait(v, nt_done, (b - 1) * 3)
                    V.tensor_tensor(other[:, q], dst_t[:, q, :].unsqueeze(2).broadcast_to([128, TILES, NB]),
                                    ids[:, q, :].unsqueeze(1).broadcast_to([128, TILES, NB]), ALU.not_equal).then_inc(other_ready[q], 1)
                elif what == "scores":
                    v.drain()
                    v.wait_ge(gathered[q], i * (16 * TILES) + 16 * TILES)
                    V.tensor_tensor(t_edge[:, q, :], rows[:, q, :, F + 1], s_edge[:], ALU.add)
                    v.drain()
                    V.scalar_tensor_tensor(out=masked[:], in0=other[:, q], scalar=-FAR,
                                           in1=t_edge[:, q, :].unsqueeze(2).broadcast_to([128, TILES, NB]), op0=ALU.mult, op1=ALU.add)
                    v.drain()
                    V.tensor_reduce(colmax[:], masked.rearrange("p j n -> p n j"), AX.X, ALU.max).then_inc(colmax_ready, 1)
                elif what == "nodemax":
                    v.wait_ge(colmax_turned, b + 1)
                    V.tensor_reduce(node_t[:, 0:1], p_att[0:NB, 0:128], AX.X, ALU.max)
                    V.tensor_copy(node6[:, 0:3], sdst3[:, bass.ds(b, 1), :].rearrange("p o k -> p (o k)"))
                    v.drain()
                    V.tensor_tensor(node_t[:, 1:2], node_t[:, 0:1], sdst[:, bass.ds(b, 1)], ALU.add)
                    v.drain()
                    V.scalar_tensor_tensor(out=node_t[:, 2:3], in0=node_t[:, 1:2], scalar=ALPHA, in1=node_t[:, 1:2],
                                           op0=ALU.mult, op1=ALU.max)
                    v.drain()
                    V.tensor_copy(node6[:, 3:4], node_t[:, 2:3])
                    v.drain()
                    V.tensor_tensor(node_t[:, 3:4], node_t[:, 2:3], node6[:, 3:4], ALU.subtract)
                    v.drain()
                    V.tensor_copy(node6[:, 4:5], node_t[:, 3:4])
                    v.drain()
                    V.tensor_tensor(node6[:, 5:6], node_t[:, 3:4], node6[:, 4:5], ALU.subtract).then_inc(node_ready, 1)
                elif what == "spread":
                    v.wait_ge(spread_done, b + 1)
                    V.tensor_reduce(spread[:], p_att[:, 128:128 + 6 * TILES].rearrange("p (j v k) -> p j v k", v=2, k=3),
                                    AX.X, ALU.add)
                    v.drain()
                    V.tensor_tensor(logit[:], t_edge[:, q, :], spread[:, :, 0], ALU.add)
                    v.drain()
                    V.scalar_tensor_tensor(out=score[:], in0=logit[:], scalar=ALPHA, in1=logit[:], op0=ALU.mult, op1=ALU.max)
                    v.drain()
                    V.tensor_tensor(logit[:], score[:], spread[:, :, 1], ALU.subtract)
                    v.drain()
                    V.tensor_scalar(score[:], logit[:], 0.0, None, ALU.min).then_inc(score_ready, 1)
                elif what == "weights":
                    v.wait_ge(exp_ready, b + 1)
                    wait(v, agg_done, b)
                    V.scalar_tensor_tensor(out=wgt[:], in0=other[:, q], scalar=0.0,
                                           in1=ex[:].unsqueeze(2).broadcast_to([128, TILES, NB]),
                                           op0=ALU.is_equal, op1=ALU.mult).then_inc(wgt_ready, 1)
                elif what == "aggregate":
                    v.wait_ge(agg_done, b + 1)
                    wait(v, agg_turned, b)
                    V.tensor_scalar(den[:, 0:1], p_agg[0:NB, F:F + 1], 1e-30, None, ALU.max)
                    v.drain()
                    V.reciprocal(den[:, 1:2], den[:, 0:1])
                    v.drain()
                    V.tensor_scalar(agg[:], p_agg[0:NB, 0:F], den[:, 1:2], None, ALU.mult).then_inc(agg_ready, 1)
                elif what == "project":
                    v.wait_ge(projected, b + 1)
                    v.wait_ge(x_loaded[q], i * 16 + 16)
                    V.tensor_tensor(x1[:, q, :], p_mix[0:NB, F:2 * F], x_in[:, q, :], ALU.add).then_inc(x1_ready, 1)
                elif what == "moments":
                    v.drain()
                    for z in range(2):
                        V.bn_stats(ln6[:, z, :], x1[:, z, :])
                    v.drain()
                    for z in range(2):
                        last = V.bn_aggr(lnmv[:, z, :], ln6[:, z, :])
                    last.then_inc(moments_ready, 1)
                elif what == "normalise":
                    v.wait_ge(lnstd_ready, i + 1)
                    wait(v, x_turned, i)
                    V.reciprocal(lnr[:], lnstd[:])
                    v.drain()
                    for z in range(2):
                        last = V.tensor_scalar(xn[:, z, :], x1[:, z, :], lnmv[:, z, 0:1], lnr[:, z:z + 1], ALU.subtract, ALU.mult)
                    last.then_inc(xn_ready, 1)
                elif what == "route":
                    v.wait_ge(routed, i + 1)
                    V.tensor_reduce(r_negmax[:], p_mix[0:NB, 0:2 * EXPERTS].rearrange("p (q e) -> p q e", q=2), AX.X, ALU.max,
                                    negate=True).then_inc(negmax_ready, 1)
                elif what == "gates":
                    v.wait_ge(r_exp_ready, i + 1)
                    V.reciprocal(r_inv[:], r_sum[:])
                    v.drain()
                    for z in range(2):
                        last = V.tensor_scalar(r_w[:, z, :], r_exp[:, z, :], r_inv[:, z:z + 1], None, ALU.mult)
                    last.then_inc(r_w_ready, 1)
                elif what == "base":
                    v.wait_ge(bias_done, i + 1)
                    V.tensor_tensor(base[:], p_mix[0:NB, :].rearrange("p (q f) -> p q f", q=2), x1[:], ALU.add).then_inc(base_ready, 1)

            def experts(g, layer, e):
                if layer != 3:
                    return
                n = g * EXPERTS + e
                if e == 0:
                    v.drain()
                    V.tensor_copy(gate[:], r_w[:])
                v.drain()
                if e == 0:
                    v.wait_ge(out_stored, g * 16 + 16)
                v.wait_ge(l3_done, n + 1)
                for z in range(2):
                    last = V.scalar_tensor_tensor(out=acc[:, z, :], in0=p_l3[0:NB, z * F:(z + 1) * F], scalar=gate[:, z, e:e + 1],
                                                  in1=(base if e == 0 else acc)[:, z, :], op0=ALU.mult, op1=ALU.add)
                last.then_inc(y_added, 1)

            over_groups(v, attention, experts)

        @block.tensor
        def _(pe):
            T = nc.tensor
            pe.wait_ge(consts_ready, 1)
            pe.wait_ge(l_gnn, 48)
            for k in range(KC):
                for c in range(KC):
                    o = (k * KC + c) * 128
                    last = T.transpose(p_l1[:, o:o + 128], gw[:, c, k * 128:(k + 1) * 128], ident[:])
            last.then_inc(gwT_done, 1)
            pe.wait_ge(awide_ready, 1)
            for s in range(2):
                for c in range(KC):
                    last = T.matmul(p_l2[:, s * F:(s + 1) * F], a_wide[:, s * KC + c, :], gw[:, c, :],
                                    start=(c == 0), stop=(c == KC - 1))
            last.then_inc(u_done, 1)
            pe.wait_ge(counts_ready, 1)
            T.matmul(p_att[0:BLOCKS, 0:1], below_n[:], ones[0:PS, 0:1], start=True, stop=True).then_inc(counts_summed, 1)
            pe.wait_ge(start_ready, 1)
            T.matmul(p_att[0:1, 64:64 + BLOCKS], start_col[:], ident[0:BLOCKS, 0:BLOCKS], start=True, stop=True).then_inc(start_turned, 1)
            pe.wait_ge(bn_rows_ready, 1)
            R = EXPERTS * KC
            for n in range(4):
                last = T.transpose(p_l3[:, n * R:(n + 1) * R], bn_rows[:, n, :], ident[0:R, 0:R])
            last.then_inc(bn_turned, 1)
            pe.wait_ge(gw_copied, 1)
            pe.wait_ge(starts_ready, 1)
            pe.wait_ge(bn_cols_ready, 1)
            pe.wait_ge(l_small, 48)
            pe.wait_ge(l_w, 48)

            def attention(i, what, q):
                b = i * 2 + (q or 0)
                if what in ("nt0", "nt1", "nt2"):
                    r = int(what[2])
                    lo, hi = NT_ROUNDS[r]
                    if r == 0:
                        pe.wait_ge(other_ready[q], i + 1)
                        wait(pe, mine_ready, b * 3)
                    if r == 2:
                        pe.wait_ge(mine_ready, b * 3 + 1)
                    for j in range(lo, hi):
                        last = T.transpose(p_nt[r % 2][0:NB, (j - lo) * 128:(j - lo + 1) * 128], other[:, q, j, :], ident_b[:])
                    last.then_inc(nt_done, 1)
                elif what == "colmax":
                    pe.wait_ge(colmax_ready, b + 1)
                    wait(pe, score_ready, b)
                    T.transpose(p_att[0:NB, 0:128], colmax[:], ident[:]).then_inc(colmax_turned, 1)
                elif what == "spread":
                    pe.wait_ge(mine_ready, b * 3 + 3)
                    pe.wait_ge(node_ready, b + 1)
                    for j in range(TILES):
                        last = T.matmul(p_att[:, 128 + 6 * j:134 + 6 * j], mine_T[:, j, :], node6[:], start=True, stop=True)
                    last.then_inc(spread_done, 1)
                elif what == "aggregate":
                    pe.wait_ge(wgt_ready, b + 1)
                    wait(pe, agg_ready, b)
                    for j in range(TILES):
                        last = T.matmul(p_agg[0:NB, 0:F + 1], wgt[:, j, :], rows[:, q, j, 0:F + 1], start=(j == 0), stop=(j == TILES - 1))
                    last.then_inc(agg_done, 1)
                elif what == "turn":
                    pe.wait_ge(agg_ready, b + 1)
                    if q == 0:
                        wait(pe, base_ready, i)
                    else:
                        pe.wait_ge(x1_ready, b)
                    for c in range(KC):
                        last = T.transpose(p_mix[:, c * NB:(c + 1) * NB], agg[:, c * 128:(c + 1) * 128], ident[0:NB, 0:NB])
                    last.then_inc(agg_turned, 1)
                elif what == "project":
                    pe.wait_ge(aggT_ready, b + 1)
                    for c in range(KC):
                        last = T.matmul(p_mix[0:NB, F:2 * F], aggT[:, c, :], gwT[:, c, :], start=(c == 0), stop=(c == KC - 1))
                    last.then_inc(projected, 1)
                elif what == "turn_x":
                    pe.wait_ge(xn_ready, i + 1)
                    pe.wait_ge(x1_ready, i * 2 + 2)
                    for c in range(KC):
                        for z in range(2):
                            o = (c * 2 + z) * NB
                            last = T.transpose(p_mix[:, o:o + NB], xn[:, z, c * 128:(c + 1) * 128], ident[0:NB, 0:NB])
                    last.then_inc(x_turned, 1)
                elif what == "route":
                    pe.wait_ge(xT_ready, i + 1)
                    for z in range(2):
                        o = p_mix[0:NB, z * EXPERTS:(z + 1) * EXPERTS]
                        for c in range(KC):
                            T.matmul(o, xT[:, c, z * NB:(z + 1) * NB], wr[:, c, :], start=(c == 0), stop=False)
                        last = T.matmul(o, ones[0:1, 0:NB], br_row[:], start=False, stop=True)
                    last.then_inc(routed, 1)
                elif what == "turn_w":
                    pe.wait_ge(r_w_ready, i + 1)
                    for z in range(2):
                        last = T.transpose(p_mix[0:EXPERTS, z * NB:(z + 1) * NB], r_w[:, z, :], ident[0:NB, 0:NB])
                    last.then_inc(w_turned, 1)
                elif what == "base":
                    pe.wait_ge(wT_ready, i + 1)
                    for z in range(2):
                        last = T.matmul(p_mix[0:NB, z * F:(z + 1) * F], r_wT[:, z * NB:(z + 1) * NB], bo_sb[:], start=True, stop=True)
                    last.then_inc(bias_done, 1)

            def experts(g, layer, e):
                n = g * EXPERTS + e
                if layer == 1:
                    if e == 0:
                        pe.wait_ge(xT_ready, g + 1)
                    pe.wait_ge(h1_ready, n + 1)
                    for m in range(KC):
                        for c in range(KC):
                            last = T.matmul(p_l1[:, m * 2 * NB:(m + 1) * 2 * NB], w1[:, e * KC + c, m * 128:(m + 1) * 128], xT[:, c, :],
                                            start=(c == 0), stop=(c == KC - 1))
                    last.then_inc(l1_done, 1)
                elif layer == 2:
                    pe.wait_ge(h2_ready, n + 1)
                    pe.wait_ge(h1_ready, n + 2)
                    for m in range(KC):
                        for c in range(KC):
                            last = T.matmul(p_l2[:, m * 2 * NB:(m + 1) * 2 * NB], w2[:, e * KC + c, m * 128:(m + 1) * 128], h1[:, e % 2, c, :],
                                            start=(c == 0), stop=(c == KC - 1))
                    last.then_inc(l2_done, 1)
                else:
                    pe.wait_ge(y_added, n + 1)
                    pe.wait_ge(h2_ready, n + 2)
                    for z in range(2):
                        for c in range(KC):
                            last = T.matmul(p_l3[0:NB, z * F:(z + 1) * F], h2[:, e % 2, c, z * NB:(z + 1) * NB], wo[:, e * KC + c, :],
                                            start=(c == 0), stop=(c == KC - 1))
                    last.then_inc(l3_done, 1)

            over_groups(pe, attention, experts)


_INS = ['x', 'src', 'dst', 'edge_attr_64', 'L0_gnn_W', 'L0_gnn_A', 'L0_ffn_Wr', 'L0_ffn_br', 'L0_ffn_W1', 'L0_ffn_b1',
        'L0_ffn_g1', 'L0_ffn_be1', 'L0_ffn_m1', 'L0_ffn_v1', 'L0_ffn_W2', 'L0_ffn_b2', 'L0_ffn_g2', 'L0_ffn_be2',
        'L0_ffn_m2', 'L0_ffn_v2', 'L0_ffn_Wo', 'L0_ffn_bo']


def kernel(**inputs):
    import numpy as _np
    import concourse.bacc as _bacc
    from concourse.bass_utils import run_bass_kernel_spmd as _run

    nc = _bacc.Bacc("TRN2", target_bir_lowering=False, num_devices=1)
    arrays, args = {}, []
    for name in _INS:
        a = _np.ascontiguousarray(inputs[name])
        arrays[f"in_{name}_dram"] = a
        args.append(nc.dram_tensor(f"in_{name}_dram", a.shape, mybir.dt.from_np(a.dtype), kind="ExternalInput").ap())
    out = nc.dram_tensor("out_dram", (NODES, F), F32, kind="ExternalOutput").ap()
    gnn_ffn_program(nc, *args, out)
    r = _run(nc, [arrays], core_ids=[0])
    return _np.asarray(r.results[0]["out_dram"])
```

```python
from contextlib import ExitStack

import concourse.bass as bass
from concourse import mybir

F32 = mybir.dt.float32
F32R = mybir.dt.float32r
BF16 = mybir.dt.bfloat16
I32 = mybir.dt.int32
U32 = mybir.dt.uint32
ALU = mybir.AluOpType
ACT = mybir.ActivationFunctionType
AX = mybir.AxisListType

NODES, EDGES, F, EDIM, EXPERTS = 6250, 100000, 256, 64, 8
NB = 125
NB_HALF = (NB + 1) // 2
BLOCKS = NODES // NB
GROUPS = BLOCKS // 2
TILES = 17
CAP = TILES * 128
ROW = F + 2
KC = F // 128
SPAN = 32
ROWS_D = EDGES // SPAN
PS = 125
CB = 5
CHUNKS = BLOCKS // CB
ALPHA, LN_EPS, BN_EPS = 0.2, 1e-5, 1e-3
FAR = 1e30
HI, LO = 0, 1
STAGED = 6
PRODUCTS = ((HI, HI), (HI, LO), (LO, HI))
NT_ROUNDS = [(0, 6), (6, 12), (12, 17)]

SLOTS = 24
FRAMES = 3
BLOCK_STEPS = {
    "edges": 0, "nt0": 1, "scores0": 1, "nt1": 1, "nt2": 2, "scores1": 2, "colmax": 4, "nodemax": 5, "spread": 6,
    "score": 7, "exp": 7, "weights": 8, "aggregate0": 10, "aggregate1": 11, "aggregate2": 12, "den": 13, "scale": 13,
    "turn": 14, "turned": 14, "project": 15, "residual": 16,
}
GROUP_STEPS = {
    "moments": 28, "std": 28, "normalise": 29, "turn_x": 30, "x_hi": 30, "x_lo": 31, "route": 32, "route_max": 33,
    "route_exp": 33, "gates": 34, "turn_w": 35, "turned_w": 35, "bias": 36, "base": 37,
}
AGG_PARTS = [(0, 6), (6, 12), (12, 17)]
FIRST_LAYER = {1: 32, 2: 36, 3: 40}


def timetable():
    steps, layers = {}, {}
    for name, slot in BLOCK_STEPS.items():
        for q in range(2):
            steps.setdefault(slot + q * (SLOTS // 2), []).append((name, q))
    for name, slot in GROUP_STEPS.items():
        steps.setdefault(slot, []).append((name, 0))
    for layer, slot in FIRST_LAYER.items():
        for e in range(EXPERTS):
            layers[slot + 3 * e] = (layer, e)
    return steps, layers


STEPS, LAYERS = timetable()


def gnn_ffn_program(nc, x, src, dst, edge_attr, gnn_W, gnn_A, Wr, br, W1, b1, g1, be1, m1, v1,
                    W2, b2, g2, be2, m2, v2, Wo, bo, out):
    table = nc.dram_tensor("table", (NODES, ROW), F32, kind="Internal").ap()
    dst_rows = dst.rearrange("(r s) -> r s", s=SPAN)
    x_blocks = x.rearrange("(b p) f -> p b f", p=NB)
    table_blocks = table.rearrange("(b p) f -> p b f", p=NB)

    with ExitStack() as ctx:
        def sb(name, shape, dt=F32):
            return ctx.enter_context(nc.sbuf_tensor(name, shape, dt))

        def sem(name):
            return ctx.enter_context(nc.semaphore(name))

        def pair(name):
            return [sem(f"{name}{q}") for q in range(2)]

        def bank(name, dt=F32):
            return ctx.enter_context(nc.psum_tensor(name, [128, 2048 // (2 if dt == BF16 else 4)], dt))

        w1 = sb("w1", [128, 2, EXPERTS * KC, F], F32R)
        w2 = sb("w2", [128, 2, EXPERTS * KC, F], F32R)
        wo = sb("wo", [128, 2, EXPERTS * KC, F], F32R)
        gwT = sb("gwT", [128, KC, F])
        a_cols = sb("a_cols", [128, 2 * KC])
        a_e = sb("a_e", [128, EDIM])
        wr = sb("wr", [128, KC, EXPERTS])
        br_row = sb("br_row", [1, EXPERTS])
        bo_sb = sb("bo_sb", [EXPERTS, F])
        bn_cols = sb("bn_cols", [128, 4, EXPERTS * KC])
        ident = sb("ident", [128, 128])
        ident_b = sb("ident_b", [128, 128], BF16)
        ones = sb("ones", [128, 128])
        eps_ln = sb("eps_ln", [128, 1])
        eps_bn = sb("eps_bn", [128, 1])
        bound_row_i = sb("bound_row_i", [128, BLOCKS], I32)
        bound_row = sb("bound_row", [128, BLOCKS])
        bound_col_i = sb("bound_col_i", [BLOCKS, 1], I32)
        bound_col = sb("bound_col", [BLOCKS, 1])
        below_n = sb("below_n", [PS, BLOCKS])
        row_f = sb("row_f", [BLOCKS, 1])
        row_i = sb("row_i", [BLOCKS, 1], I32)
        in_row_n = sb("in_row_n", [BLOCKS, 1])
        start_col = sb("start_col", [BLOCKS, 1])
        starts = sb("starts", [1, BLOCKS], I32)
        mv = sb("mv", [NB, 2, CB, 2])
        std = sb("std", [NB, 2, CB])
        rstd = sb("rstd", [NB, 2, CB])
        nmr = sb("nmr", [NB, 2, CB])
        dots = sb("dots", [NB, 2, 2, CB])
        sdst = sb("sdst", [NB, BLOCKS])
        sdst_r = sb("sdst_r", [NB, BLOCKS])
        sdst3 = sb("sdst3", [NB, BLOCKS, 3], BF16)
        node_ids = sb("node_ids", [128, NB, TILES], BF16)
        block_base = sb("block_base", [128, 2])
        two_blocks = sb("two_blocks", [128, 1])
        dst_l = sb("dst_l", [128, TILES], BF16)
        src_t = sb("src_t", [128, 2, TILES], I32)
        dst_t = sb("dst_t", [128, 2, TILES], I32)
        attr = sb("attr", [128, 2, TILES, EDIM])
        rows = sb("rows", [128, 2, TILES, ROW])
        early = rows.rearrange("p q j f -> p (q j f)")
        XC, TR = 2 * CB * F, 2 * CB * ROW
        xc = early[0:NB, 0:XC].rearrange("p (q b f) -> p q b f", q=2, b=CB)
        tr = early[0:NB, XC:XC + TR].rearrange("p (q b f) -> p q b f", q=2, b=CB)
        s_edge = sb("s_edge", [128, TILES])
        t_edge = sb("t_edge", [128, 2, TILES])
        other = sb("other", [128, 2, NB, TILES], BF16)
        masked = sb("masked", [128, NB_HALF, TILES])
        colmax = sb("colmax", [128, NB])
        mine_T = sb("mine_T", [NB, TILES, 128], BF16)
        node_t = sb("node_t", [NB, 4])
        node6 = sb("node6", [NB, 6], BF16)
        spread = sb("spread", [128, TILES, 2])
        logit = sb("logit", [128, TILES])
        score = sb("score", [128, TILES])
        ex = sb("ex", [128, TILES])
        wgt = sb("wgt", [128, TILES, NB])
        den = sb("den", [NB, 2])
        aggT = sb("aggT", [128, KC, NB])
        x1 = sb("x1", [NB, 2, F])
        ln6 = sb("ln6", [NB, 2, 6])
        lnmv = sb("lnmv", [NB, 2, 2])
        lnstd = sb("lnstd", [NB, 2])
        lnr = sb("lnr", [NB, 2])
        xn = sb("xn", [NB, 2, F])
        xT = sb("xT", [128, 2, KC, 2 * NB], F32R)
        r_negmax = sb("r_negmax", [NB, 2])
        r_exp = sb("r_exp", [NB, 2, EXPERTS])
        r_sum = sb("r_sum", [NB, 2])
        r_inv = sb("r_inv", [NB, 2])
        r_w = sb("r_w", [NB, 2, EXPERTS])
        r_wT = aggT.rearrange("p c n -> p (c n)")[0:EXPERTS, :]
        gate = sb("gate", [NB, 2, EXPERTS])
        base = xn
        agg = wgt.rearrange("p j n -> p (j n)")[0:NB, 0:F]
        h1 = sb("h1", [128, 2, 2, KC, 2 * NB], F32R)
        h2 = sb("h2", [128, 2, 2, KC, 2 * NB], F32R)
        h_mem = sb("h_mem", [128, 2, 512])
        h_full = h_mem[:, :, 0:KC * 2 * NB].rearrange("p l (c n) -> p l c n", c=KC)
        acc = sb("acc", [NB, 2, F])

        gw = h_mem[:, 0, :].rearrange("p (c f) -> p c f", c=KC)
        a_wide = h_mem[:, 1, :].rearrange("p (k n) -> p k n", k=2 * KC)
        junk = xn
        w_staged = early[:, XC + TR:XC + TR + STAGED * KC * F].rearrange("p (n c f) -> p n c f", n=STAGED, c=KC)
        ids_i = early[:, XC + TR:XC + TR + NB * TILES].bitcast(I32)
        R = EXPERTS * KC
        wgt_mem = wgt.rearrange("p j n -> p (j n)")
        bn = wgt_mem[0:R, 0:16 * 128].rearrange("p (k n) -> p k n", n=128)
        bn_in, bn_tmp, bn_rows = bn[:, 0:10], bn[:, 10:12], bn[:, 12:16]
        st6 = wgt_mem[0:NB, 16 * 128:16 * 128 + 12 * CB].rearrange("p (q b k) -> p q b k", q=2, k=6)
        masked_mem = masked.rearrange("p n j -> p (n j)")
        SAMPLES = EDGES // PS // SPAN
        HALF = BLOCKS * SAMPLES // 2
        below = masked_mem[0:PS, 0:HALF].bitcast(BF16).rearrange("p (b n) -> p b n", b=BLOCKS)
        window = masked_mem[0:BLOCKS, HALF:HALF + SPAN].bitcast(I32)
        in_row = masked_mem[0:BLOCKS, HALF + SPAN:HALF + 2 * SPAN]
        dst_all = mine_T.rearrange("p j e -> p (j e)")[0:PS, 0:2 * EDGES // PS].bitcast(I32)
        u_rows = acc

        p_agg = bank("p_agg")
        p_nt = [bank("p_nt0", BF16), bank("p_nt1", BF16)]
        p_att = bank("p_att")
        p_mix = bank("p_mix")
        p_l1 = bank("p_l1")
        p_l2 = bank("p_l2")
        p_l3 = bank("p_l3")

        l_gnn = sem("l_gnn")
        l_dst = sem("l_dst")
        l_bn = sem("l_bn")
        l_small = sem("l_small")
        l_w = sem("l_w")
        w_hi_ready = sem("w_hi_ready")
        w_split = sem("w_split")
        l_x = pair("l_x")
        consts_ready = sem("consts_ready")
        gwT_done = sem("gwT_done")
        awide_ready = sem("awide_ready")
        u_done = sem("u_done")
        gw_copied = sem("gw_copied")
        counts_ready = sem("counts_ready")
        counts_summed = sem("counts_summed")
        row_ready = sem("row_ready")
        window_loaded = sem("window_loaded")
        start_ready = sem("start_ready")
        start_turned = sem("start_turned")
        starts_ready = sem("starts_ready")
        bn_var_ready = sem("bn_var_ready")
        bn_rows_ready = sem("bn_rows_ready")
        bn_turned = sem("bn_turned")
        bn_cols_ready = sem("bn_cols_ready")
        stats_ready = sem("stats_ready")
        std_ready = sem("std_ready")
        rstd_ready = sem("rstd_ready")
        table_rows = sem("table_rows")
        table_dots = sem("table_dots")
        table_stored = pair("table_stored")
        edges_loaded = pair("edges_loaded")
        x_loaded = pair("x_loaded")
        products_ready = pair("products_ready")
        gathered = pair("gathered")
        other_ready = pair("other_ready")
        nt_done = sem("nt_done")
        mine_ready = sem("mine_ready")
        half_ready = sem("half_ready")
        colmax_ready = sem("colmax_ready")
        colmax_turned = sem("colmax_turned")
        node_ready = sem("node_ready")
        spread_done = sem("spread_done")
        score_ready = sem("score_ready")
        exp_ready = sem("exp_ready")
        wgt_ready = sem("wgt_ready")
        agg_done = sem("agg_done")
        den_ready = sem("den_ready")
        agg_ready = sem("agg_ready")
        agg_turned = sem("agg_turned")
        aggT_ready = sem("aggT_ready")
        projected = sem("projected")
        x1_ready = sem("x1_ready")
        moments_ready = sem("moments_ready")
        lnstd_ready = sem("lnstd_ready")
        xn_ready = sem("xn_ready")
        x_turned = sem("x_turned")
        xT_hi_ready = sem("xT_hi_ready")
        xT_ready = sem("xT_ready")
        routed = sem("routed")
        negmax_ready = sem("negmax_ready")
        r_exp_ready = sem("r_exp_ready")
        r_w_ready = sem("r_w_ready")
        w_turned = sem("w_turned")
        wT_ready = sem("wT_ready")
        bias_done = sem("bias_done")
        base_ready = sem("base_ready")
        l1_done = sem("l1_done")
        h1_full = sem("h1_full")
        h1_hi_ready = sem("h1_hi_ready")
        h1_ready = sem("h1_ready")
        l2_done = sem("l2_done")
        h2_full = sem("h2_full")
        h2_hi_ready = sem("h2_hi_ready")
        h2_ready = sem("h2_ready")
        l3_done = sem("l3_done")
        y_added = sem("y_added")
        out_stored = sem("out_stored")

        def wait(eng, semaphore, value):
            if not isinstance(value, int) or value > 0:
                eng.wait_ge(semaphore, value)

        def over_groups(eng, attention, experts, behind=0):
            def frame(i, ages):
                for s in range(SLOTS):
                    for age in ages:
                        if s + age * SLOTS - behind in LAYERS:
                            experts(i - age, *LAYERS[s + age * SLOTS - behind])
                    for age in ages:
                        for what, q in STEPS.get(s + age * SLOTS, []):
                            attention(i - age, what, q)
            frame(0, (0,))
            frame(1, (1, 0))
            with eng.Fori(FRAMES - 1, GROUPS) as i:
                frame(i, (2, 1, 0))
            frame(GROUPS, (2, 1))
            frame(GROUPS + 1, (2,))

        block = ctx.enter_context(nc.Block())

        @block.sync
        def _(sp):
            sp.dma_start(gw, gnn_W.rearrange("(c p) f -> p c f", p=128)).then_inc(l_gnn, 16)
            sp.dma_start(a_cols[:], gnn_A[0, 0:2 * F].rearrange("(c p) -> p c", p=128), allow_slow_non_contiguous=True).then_inc(l_gnn, 16)
            sp.dma_start(a_e[:], gnn_A[0:1, 2 * F:2 * F + EDIM].broadcast_to([128, EDIM])).then_inc(l_gnn, 16)
            sp.dma_start(xc[:, 0], x_blocks[:, 0:CB, :]).then_inc(l_x[0], 16)
            sp.dma_start(dst_all, dst.rearrange("(p n) -> p n", p=PS)).then_inc(l_dst, 16)
            sp.dma_start(xc[:, 1], x_blocks[:, CB:2 * CB, :]).then_inc(l_x[1], 16)
            for n, a in enumerate((b1, g1, be1, m1, v1, b2, g2, be2, m2, v2)):
                sp.dma_start(bn_in[:, n, :], a.rearrange("e (c p) -> (e c) p", p=128)).then_inc(l_bn, 16)
            sp.dma_start(wr[:], Wr.rearrange("(c p) e -> p c e", p=128)).then_inc(l_small, 16)
            sp.dma_start(br_row[:], br.rearrange("(o e) -> o e", o=1)).then_inc(l_small, 16)
            sp.dma_start(bo_sb[:], bo).then_inc(l_small, 16)

            def store_rows(c, q, last=False):
                sp.wait_ge(table_dots, c + 1)
                sp.dma_start(table_blocks[:, bass.ds(c * CB, CB), :], tr[:, q]).then_inc(table_stored[q], 16)
                if not last:
                    sp.dma_start(xc[:, q], x_blocks[:, bass.ds(c * CB + 2 * CB, CB), :]).then_inc(l_x[q], 16)

            sp.wait_ge(consts_ready, 1)
            with sp.Fori(0, CHUNKS // 2 - 1) as i:
                sp.wait_ge(w_split, i * STAGED)
                for n in range(STAGED):
                    w, k = (W1, W2, Wo)[n % 3], n // 3
                    sp.dma_start(w_staged[:, n], w[bass.ds(i * 2 + k, 1)].rearrange("e (c p) f -> p (e c) f", p=128)).then_inc(l_w, 16)
                for q in range(2):
                    store_rows(i * 2 + q, q)
            for q in range(2):
                store_rows(CHUNKS - 2 + q, q, last=True)
            sp.wait_ge(starts_ready, 1)

            def load_edges(i, q):
                first = sp.value_load(starts[0:1, bass.ds(i * 2 + q, 1)], min_val=0, max_val=EDGES - CAP)
                for t, of in ((src_t, src), (dst_t, dst)):
                    sp.dma_start(t[:, q, :], of[bass.ds(first, CAP)].rearrange("(p j) -> p j", j=TILES)).then_inc(edges_loaded[q], 16)
                sp.dma_start(attr[:, q], edge_attr[bass.ds(first, CAP), :].rearrange("(p j) d -> p j d", j=TILES)).then_inc(edges_loaded[q], 16)

            def load_x(i, q):
                sp.dma_start(x1[:, q, :], x[bass.ds(i * (2 * NB) + q * NB, NB), :]).then_inc(x_loaded[q], 16)

            def store_out(g):
                sp.wait_ge(y_added, g * EXPERTS + EXPERTS + 1)
                sp.dma_start(out[bass.ds(g * (2 * NB), 2 * NB), :].rearrange("(q p) f -> p q f", p=NB), acc[:]).then_inc(out_stored, 16)

            def next_edges(i):
                for q in range(2):
                    sp.wait_ge(gathered[q], i * (16 * TILES))
                    sp.wait_ge(other_ready[q], i)
                    load_edges(i, q)

            def next_x(i):
                sp.wait_ge(base_ready, i)
                for q in range(2):
                    load_x(i, q)

            for q in range(2):
                load_edges(0, q)
                load_x(0, q)
            next_edges(1)
            next_edges(2)
            next_x(1)
            with sp.Fori(2, GROUPS - 1) as i:
                next_edges(i + 1)
                next_x(i)
                store_out(i - 2)
            next_x(GROUPS - 1)
            for g in range(GROUPS - 3, GROUPS):
                store_out(g)
            sp.wait_ge(out_stored, 16 * (GROUPS + 1))

        @block.gpsimd
        def _(pool):
            nc.gpsimd.memset(ones[:], 1.0)
            nc.gpsimd.memset(ident[:], 0.0)
            nc.gpsimd.memset(eps_ln[:], LN_EPS)
            nc.gpsimd.memset(eps_bn[:], BN_EPS)
            nc.gpsimd.memset(two_blocks[:], float(2 * NB))
            for q in range(2):
                nc.gpsimd.memset(block_base[:, q:q + 1], float(NB * q - 2 * NB))
            nc.gpsimd.iota(bound_row_i[:], pattern=[[NB, BLOCKS]], base=0, channel_multiplier=0)
            nc.gpsimd.iota(bound_col_i[:], pattern=[[0, 1]], base=0, channel_multiplier=NB)
            nc.gpsimd.iota(ids_i, pattern=[[1, NB], [0, TILES]], base=0, channel_multiplier=0)
            pool.drain()
            nc.gpsimd.affine_select(out=ident[:], in_=ident[:], compare_op=ALU.not_equal, fill=1.0, base=0,
                                    pattern=[[-1, 128]], channel_multiplier=1)
            nc.gpsimd.tensor_copy(bound_row[:], bound_row_i[:])
            nc.gpsimd.tensor_copy(bound_col[:], bound_col_i[:])
            nc.gpsimd.tensor_copy(node_ids.rearrange("p n j -> p (n j)"), ids_i)
            pool.drain()
            nc.gpsimd.tensor_copy(ident_b[:], ident[:]).then_inc(consts_ready, 1)

            def split_weights(i):
                for n in range(STAGED):
                    pool.wait_ge(l_w, i * (16 * STAGED) + 16 * STAGED)
                    w, k = (w1, w2, wo)[n % 3], n // 3
                    e = bass.ds(i * (2 * KC) + k * KC, KC)
                    nc.gpsimd.tensor_copy(w[:, HI, e], w_staged[:, n]).then_inc(w_hi_ready, 1)
                    pool.wait_ge(w_hi_ready, i * STAGED + n + 1)
                    nc.gpsimd.tensor_tensor(w[:, LO, e], w_staged[:, n], w[:, HI, e].bitcast(F32), ALU.subtract).then_inc(w_split, 1)

            pool.wait_ge(row_ready, 1)
            nc.gpsimd.indirect_dma_start(window, None, dst_rows, bass.IndirectOffsetOnAxis(ap=row_i[:].bitcast(U32), axis=0)).then_inc(window_loaded, 16)
            with pool.Fori(0, EXPERTS // 2) as i:
                split_weights(i)
            pool.wait_ge(w_split, 3 * EXPERTS)
            for q in range(2):
                pool.wait_ge(table_stored[q], 16 * (CHUNKS // 2))

            def gather(i, q):
                wait(pool, other_ready[q], i)
                pool.wait_ge(edges_loaded[q], i * 48 + 48)
                nc.gpsimd.tensor_tensor(block_base[:, q:q + 1], block_base[:, q:q + 1], two_blocks[:], ALU.add)
                wait(pool, agg_done, i * 2 + q - 1)
                nc.gpsimd.tensor_tensor(attr[:, q], attr[:, q], a_e[:].unsqueeze(1).broadcast_to([128, TILES, EDIM]),
                                        ALU.mult).then_inc(products_ready[q], 1)
                for j in range(TILES):
                    nc.gpsimd.indirect_dma_start(
                        rows[:, q, j, :], None, table,
                        bass.IndirectOffsetOnAxis(ap=src_t[:, q, j:j + 1].bitcast(U32), axis=0)).then_inc(gathered[q], 16)

            for q in range(2):
                gather(0, q)
            with pool.Fori(1, GROUPS) as i:
                for q in range(2):
                    gather(i, q)

        @block.scalar
        def _(act):
            act.nop().then_inc(h1_ready, 1)
            act.nop().then_inc(h2_ready, 1)
            act.nop().then_inc(out_stored, 16)
            act.wait_ge(consts_ready, 1)
            act.wait_ge(l_bn, 160)
            for l in range(2):
                last = nc.scalar.activation(bn_tmp[:, l, :], bn_in[:, 5 * l + 4, :], ACT.Sqrt, bias=eps_bn[0:EXPERTS * KC, :])
            last.then_inc(bn_var_ready, 1)

            def table_chunk(c, q):
                act.wait_ge(stats_ready, c + 1)
                nc.scalar.activation(std[:, q, :], mv[:, q, :, 1], ACT.Sqrt, bias=eps_ln[0:NB, :]).then_inc(std_ready, 1)
                act.wait_ge(rstd_ready, c + 1)
                wait(act, table_stored[q], (c - q) * 8)
                for b in range(CB):
                    last = nc.scalar.activation(tr[:, q, b, 0:F], xc[:, q, b, :], ACT.Identity,
                                                bias=nmr[:, q, b:b + 1], scale=rstd[:, q, b:b + 1])
                last.then_inc(table_rows, 1)

            for q in range(2):
                table_chunk(q, q)
            with act.Fori(1, CHUNKS // 2) as i:
                for q in range(2):
                    table_chunk(i * 2 + q, q)

            def attention(i, what, q):
                b = i * 2 + q
                if what in ("nt0", "nt1", "nt2"):
                    r = int(what[2])
                    lo, hi = NT_ROUNDS[r]
                    act.wait_ge(nt_done, b * 3 + r + 1)
                    if r == 0:
                        wait(act, spread_done, b)
                    nc.scalar.activation(mine_T[:, lo:hi, :].rearrange("p j e -> p (j e)"),
                                         p_nt[(r) % 2][0:NB, 0:(hi - lo) * 128], ACT.Copy, bias=1.0, scale=-1.0).then_inc(mine_ready, 1)
                elif what == "exp":
                    act.wait_ge(score_ready, b + 1)
                    wait(act, wgt_ready, b)
                    nc.scalar.activation(ex[:], score[:], ACT.Exp).then_inc(exp_ready, 1)
                elif what == "scale":
                    act.wait_ge(den_ready, b + 1)
                    wait(act, agg_turned, b)
                    nc.scalar.activation(agg, p_agg[0:NB, 0:F], ACT.Copy, scale=den[:, 1:2]).then_inc(agg_ready, 1)
                elif what == "turned":
                    act.wait_ge(agg_turned, b + 1)
                    nc.scalar.activation(aggT.rearrange("p c n -> p (c n)"), p_mix[:, 0:KC * NB], ACT.Copy).then_inc(aggT_ready, 1)
                elif what == "std":
                    act.wait_ge(moments_ready, i + 1)
                    nc.scalar.activation(lnstd[:], lnmv[:, :, 1], ACT.Sqrt, bias=eps_ln[0:NB, :]).then_inc(lnstd_ready, 1)
                elif what == "x_hi":
                    act.wait_ge(x_turned, i + 1)
                    nc.scalar.activation(xT[:, HI].rearrange("p c n -> p (c n)"), p_mix[:, 0:KC * 2 * NB], ACT.Copy).then_inc(xT_hi_ready, 1)
                elif what == "route_exp":
                    act.wait_ge(negmax_ready, i + 1)
                    for z in range(2):
                        last = nc.scalar.activation(r_exp[:, z, :], p_mix[0:NB, z * EXPERTS:(z + 1) * EXPERTS], ACT.Exp,
                                                    bias=r_negmax[:, z:z + 1], accum_out=r_sum[:, z:z + 1])
                    last.then_inc(r_exp_ready, 1)
                elif what == "turned_w":
                    act.wait_ge(w_turned, i + 1)
                    nc.scalar.activation(r_wT, p_mix[0:EXPERTS, 0:2 * NB], ACT.Copy).then_inc(wT_ready, 1)

            def experts(g, layer, e):
                n = g * EXPERTS + e
                if layer == 3:
                    return
                done, bank_, h, full, hi_ready, lo_ready = ((l1_done, p_l1, h1, h1_full, h1_hi_ready, h1_ready),
                                                            (l2_done, p_l2, h2, h2_full, h2_hi_ready, h2_ready))[layer - 1]
                act.wait_ge(lo_ready, n + 1)
                act.wait_ge(done, n + 1)
                for m in range(KC):
                    k = e * KC + m
                    last = nc.scalar.activation(h_full[:, layer - 1, m, :], bank_[:, m * 2 * NB:(m + 1) * 2 * NB], ACT.Relu,
                                                bias=bn_cols[:, 2 * layer - 1, k:k + 1], scale=bn_cols[:, 2 * layer - 2, k:k + 1])
                last.then_inc(full, 1)
                act.wait_ge(full, n + 1)
                nc.scalar.activation(h[:, e % 2, HI], h_full[:, layer - 1], ACT.Copy).then_inc(hi_ready, 1)

            act.wait_ge(bn_cols_ready, 1)
            over_groups(act, attention, experts)

        @block.vector
        def _(v):
            V = nc.vector
            v.nop().then_inc(y_added, 1)
            V.memset(tr[:, :, :, F:F + 1], 1.0)
            v.wait_ge(l_gnn, 48)
            V.tensor_copy(a_wide, a_cols[:].unsqueeze(2).broadcast_to([128, 2 * KC, 128])).then_inc(awide_ready, 1)

            def stats(c, q):
                v.wait_ge(l_x[q], (c - q) * 8 + 16)
                for b in range(CB):
                    V.bn_stats(st6[:, q, b, :], xc[:, q, b, :])
                v.drain()
                for b in range(CB):
                    last = V.bn_aggr(mv[:, q, b, :], st6[:, q, b, :])
                last.then_inc(stats_ready, 1)

            def scale(c, q):
                v.wait_ge(std_ready, c + 1)
                V.reciprocal(rstd[:, q, :], std[:, q, :])
                v.drain()
                V.scalar_tensor_tensor(out=nmr[:, q, :], in0=mv[:, q, :, 0], scalar=-1.0, in1=rstd[:, q, :],
                                       op0=ALU.mult, op1=ALU.mult).then_inc(rstd_ready, 1)

            def dot_rows(c, q):
                v.wait_ge(table_rows, c + 1)
                for b in range(CB):
                    V.tensor_tensor_reduce(junk[:, 0, :], tr[:, q, b, 0:F], u_rows[:, 0, :], 1.0, 0.0, ALU.mult, ALU.add,
                                           dots[:, q, 0, b:b + 1])
                    V.tensor_tensor_reduce(junk[:, 1, :], tr[:, q, b, 0:F], u_rows[:, 1, :], 1.0, 0.0, ALU.mult, ALU.add,
                                           dots[:, q, 1, b:b + 1])
                    v.drain()
                V.tensor_copy(tr[:, q, :, F + 1], dots[:, q, 0, :]).then_inc(table_dots, 1)
                V.tensor_copy(sdst[:, bass.ds(c * CB, CB)], dots[:, q, 1, :])

            stats(0, 0)
            v.wait_ge(l_dst, 16)
            v.wait_ge(consts_ready, 1)
            V.tensor_tensor(below, dst_all.rearrange("p (n s) -> p n s", s=SPAN)[:, :, 0].unsqueeze(1).broadcast_to([PS, BLOCKS, SAMPLES]),
                            bound_row[0:PS, :].unsqueeze(2).broadcast_to([PS, BLOCKS, SAMPLES]), ALU.is_lt)
            v.drain()
            V.tensor_reduce(below_n[:], below, AX.X, ALU.add).then_inc(counts_ready, 1)
            v.wait_ge(gwT_done, 1)
            V.tensor_copy(gwT.rearrange("p c f -> p (c f)"), p_l1[:, :]).then_inc(gw_copied, 1)
            v.wait_ge(u_done, 1)
            V.tensor_copy(u_rows.rearrange("p s f -> p (s f)"), p_l2[0:NB, :])
            v.wait_ge(counts_summed, 1)
            V.tensor_scalar(row_f[:], p_att[0:BLOCKS, 0:1], -1.0, 0.0, ALU.add, ALU.max)
            v.drain()
            V.tensor_copy(row_i[:], row_f[:]).then_inc(row_ready, 1)
            scale(0, 0)
            stats(1, 1)
            v.wait_ge(window_loaded, 16)
            V.tensor_scalar(in_row, window, bound_col[:, 0:1], None, ALU.is_lt)
            v.drain()
            V.tensor_reduce(in_row_n[:], in_row, AX.X, ALU.add)
            v.drain()
            V.scalar_tensor_tensor(out=start_col[:], in0=row_f[:], scalar=float(SPAN), in1=in_row_n[:], op0=ALU.mult, op1=ALU.add)
            v.drain()
            V.tensor_scalar(start_col[:], start_col[:], float(EDGES - CAP), None, ALU.min).then_inc(start_ready, 1)
            v.wait_ge(bn_var_ready, 1)
            V.reciprocal(bn_tmp, bn_tmp)
            v.drain()
            for l in range(2):
                V.tensor_tensor(bn_rows[:, 2 * l, :], bn_in[:, 5 * l + 1, :], bn_tmp[:, l, :], ALU.mult)
                V.tensor_tensor(bn_rows[:, 2 * l + 1, :], bn_in[:, 5 * l, :], bn_in[:, 5 * l + 3, :], ALU.subtract)
                v.drain()
                V.tensor_tensor(bn_rows[:, 2 * l + 1, :], bn_rows[:, 2 * l + 1, :], bn_rows[:, 2 * l, :], ALU.mult)
                v.drain()
                last = V.tensor_tensor(bn_rows[:, 2 * l + 1, :], bn_rows[:, 2 * l + 1, :], bn_in[:, 5 * l + 2, :], ALU.add)
            last.then_inc(bn_rows_ready, 1)
            v.wait_ge(start_turned, 1)
            V.tensor_copy(starts[:], p_att[0:1, 64:64 + BLOCKS]).then_inc(starts_ready, 1)
            v.wait_ge(bn_turned, 1)
            V.tensor_copy(bn_cols.rearrange("p n k -> p (n k)"), p_l3[:, 0:4 * EXPERTS * KC]).then_inc(bn_cols_ready, 1)

            dot_rows(0, 0)
            with v.Fori(0, CHUNKS // 2 - 1) as i:
                for q in (1, 0):
                    c = i * 2 + (1 if q else 2)
                    scale(c, q)
                    stats(c + 1, 1 - q)
                    dot_rows(c, q)
            scale(CHUNKS - 1, 1)
            dot_rows(CHUNKS - 1, 1)
            v.drain()
            V.tensor_copy(sdst3[:, :, 0], sdst[:])
            v.drain()
            V.tensor_tensor(sdst_r[:], sdst[:], sdst3[:, :, 0], ALU.subtract)
            v.drain()
            V.tensor_copy(sdst3[:, :, 1], sdst_r[:])
            v.drain()
            V.tensor_tensor(sdst_r[:], sdst_r[:], sdst3[:, :, 1], ALU.subtract)
            v.drain()
            V.tensor_copy(sdst3[:, :, 2], sdst_r[:])

            def greatest(q, lo, hi):
                V.scalar_tensor_tensor(out=masked[:, 0:hi - lo], in0=other[:, q, lo:hi], scalar=-FAR,
                                       in1=t_edge[:, q, :].unsqueeze(1).broadcast_to([128, hi - lo, TILES]), op0=ALU.mult, op1=ALU.add)
                v.drain()
                return V.tensor_reduce(colmax[:, lo:hi], masked[:, 0:hi - lo], AX.X, ALU.max)

            def attention(i, what, q):
                b = i * 2 + q
                if what == "edges":
                    v.wait_ge(products_ready[q], i + 1)
                    V.tensor_scalar(dst_l[:], dst_t[:, q, :], block_base[:, q:q + 1], None, ALU.subtract)
                    V.tensor_reduce(s_edge[:], attr[:, q], AX.X, ALU.add)
                    v.drain()
                    wait(v, nt_done, (b - 1) * 3)
                    V.tensor_tensor(other[:, q], dst_l[:].unsqueeze(1).broadcast_to([128, NB, TILES]), node_ids[:],
                                    ALU.not_equal).then_inc(other_ready[q], 1)
                elif what == "scores0":
                    v.wait_ge(other_ready[q], i + 1)
                    v.wait_ge(gathered[q], i * (16 * TILES) + 16 * TILES)
                    V.tensor_tensor(t_edge[:, q, :], rows[:, q, :, F + 1], s_edge[:], ALU.add)
                    v.drain()
                    greatest(q, 0, NB_HALF).then_inc(half_ready, 1)
                elif what == "scores1":
                    v.wait_ge(half_ready, b + 1)
                    greatest(q, NB_HALF, NB).then_inc(colmax_ready, 1)
                elif what == "nodemax":
                    v.wait_ge(colmax_turned, b + 1)
                    V.tensor_reduce(node_t[:, 0:1], p_att[0:NB, 0:128], AX.X, ALU.max)
                    V.tensor_copy(node6[:, 0:3], sdst3[:, bass.ds(b, 1), :].rearrange("p o k -> p (o k)"))
                    v.drain()
                    V.tensor_tensor(node_t[:, 1:2], node_t[:, 0:1], sdst[:, bass.ds(b, 1)], ALU.add)
                    v.drain()
                    V.scalar_tensor_tensor(out=node_t[:, 2:3], in0=node_t[:, 1:2], scalar=ALPHA, in1=node_t[:, 1:2],
                                           op0=ALU.mult, op1=ALU.max)
                    v.drain()
                    V.tensor_copy(node6[:, 3:4], node_t[:, 2:3])
                    v.drain()
                    V.tensor_tensor(node_t[:, 3:4], node_t[:, 2:3], node6[:, 3:4], ALU.subtract)
                    v.drain()
                    V.tensor_copy(node6[:, 4:5], node_t[:, 3:4])
                    v.drain()
                    V.tensor_tensor(node6[:, 5:6], node_t[:, 3:4], node6[:, 4:5], ALU.subtract).then_inc(node_ready, 1)
                elif what == "score":
                    v.wait_ge(spread_done, b + 1)
                    V.tensor_reduce(spread[:], p_att[:, 128:128 + 6 * TILES].rearrange("p (j v k) -> p j v k", v=2, k=3),
                                    AX.X, ALU.add)
                    v.drain()
                    V.tensor_tensor(logit[:], t_edge[:, q, :], spread[:, :, 0], ALU.add)
                    v.drain()
                    V.scalar_tensor_tensor(out=score[:], in0=logit[:], scalar=ALPHA, in1=logit[:], op0=ALU.mult, op1=ALU.max)
                    v.drain()
                    V.tensor_tensor(logit[:], score[:], spread[:, :, 1], ALU.subtract)
                    v.drain()
                    V.tensor_scalar(score[:], logit[:], 0.0, None, ALU.min).then_inc(score_ready, 1)
                elif what == "weights":
                    v.wait_ge(exp_ready, b + 1)
                    wait(v, agg_turned, b)
                    V.scalar_tensor_tensor(out=wgt[:], in0=other[:, q].rearrange("p n j -> p j n"), scalar=0.0,
                                           in1=ex[:].unsqueeze(2).broadcast_to([128, TILES, NB]),
                                           op0=ALU.is_equal, op1=ALU.mult).then_inc(wgt_ready, 1)
                elif what == "den":
                    v.wait_ge(agg_done, b + 1)
                    V.tensor_scalar(den[:, 0:1], p_agg[0:NB, F:F + 1], 1e-30, None, ALU.max)
                    v.drain()
                    V.reciprocal(den[:, 1:2], den[:, 0:1]).then_inc(den_ready, 1)
                elif what == "residual":
                    v.wait_ge(projected, b + 1)
                    v.wait_ge(x_loaded[q], i * 16 + 16)
                    V.tensor_tensor(x1[:, q, :], p_mix[0:NB, F:2 * F], x1[:, q, :], ALU.add).then_inc(x1_ready, 1)
                elif what == "moments":
                    v.drain()
                    for z in range(2):
                        V.bn_stats(ln6[:, z, :], x1[:, z, :])
                    v.drain()
                    for z in range(2):
                        last = V.bn_aggr(lnmv[:, z, :], ln6[:, z, :])
                    last.then_inc(moments_ready, 1)
                elif what == "normalise":
                    v.wait_ge(lnstd_ready, i + 1)
                    wait(v, x_turned, i)
                    V.reciprocal(lnr[:], lnstd[:])
                    v.drain()
                    for z in range(2):
                        last = V.tensor_scalar(xn[:, z, :], x1[:, z, :], lnmv[:, z, 0:1], lnr[:, z:z + 1], ALU.subtract, ALU.mult)
                    last.then_inc(xn_ready, 1)
                elif what == "x_lo":
                    v.wait_ge(xT_hi_ready, i + 1)
                    V.tensor_tensor(xT[:, LO].rearrange("p c n -> p (c n)"), p_mix[:, 0:KC * 2 * NB],
                                    xT[:, HI].rearrange("p c n -> p (c n)").bitcast(F32), ALU.subtract).then_inc(xT_ready, 1)
                elif what == "route_max":
                    v.wait_ge(routed, i + 1)
                    V.tensor_reduce(r_negmax[:], p_mix[0:NB, 0:2 * EXPERTS].rearrange("p (q e) -> p q e", q=2), AX.X, ALU.max,
                                    negate=True).then_inc(negmax_ready, 1)
                elif what == "gates":
                    v.wait_ge(r_exp_ready, i + 1)
                    V.reciprocal(r_inv[:], r_sum[:])
                    v.drain()
                    for z in range(2):
                        last = V.tensor_scalar(r_w[:, z, :], r_exp[:, z, :], r_inv[:, z:z + 1], None, ALU.mult)
                    last.then_inc(r_w_ready, 1)
                elif what == "base":
                    v.wait_ge(bias_done, i + 1)
                    V.tensor_tensor(base[:], p_mix[0:NB, :].rearrange("p (q f) -> p q f", q=2), x1[:], ALU.add).then_inc(base_ready, 1)

            def experts(g, layer, e):
                n = g * EXPERTS + e
                if layer < 3:
                    h, hi_ready, ready = ((h1, h1_hi_ready, h1_ready), (h2, h2_hi_ready, h2_ready))[layer - 1]
                    v.wait_ge(hi_ready, n + 1)
                    V.tensor_tensor(h[:, e % 2, LO], h_full[:, layer - 1], h[:, e % 2, HI].bitcast(F32), ALU.subtract).then_inc(ready, 1)
                    return
                if e == 0:
                    v.wait_ge(out_stored, g * 16 + 16)
                    V.tensor_copy(gate[:], r_w[:])
                    v.drain()
                v.wait_ge(l3_done, n + 1)
                for z in range(2):
                    last = V.scalar_tensor_tensor(out=acc[:, z, :], in0=p_l3[0:NB, z * F:(z + 1) * F], scalar=gate[:, z, e:e + 1],
                                                  in1=(base if e == 0 else acc)[:, z, :], op0=ALU.mult, op1=ALU.add)
                last.then_inc(y_added, 1)

            over_groups(v, attention, experts, behind=1)

        @block.tensor
        def _(pe):
            T = nc.tensor
            pe.wait_ge(consts_ready, 1)
            pe.wait_ge(l_gnn, 48)
            for k in range(KC):
                for c in range(KC):
                    o = (k * KC + c) * 128
                    last = T.transpose(p_l1[:, o:o + 128], gw[:, c, k * 128:(k + 1) * 128], ident[:])
            last.then_inc(gwT_done, 1)
            pe.wait_ge(awide_ready, 1)
            for s in range(2):
                for c in range(KC):
                    last = T.matmul(p_l2[:, s * F:(s + 1) * F], a_wide[:, s * KC + c, :], gw[:, c, :],
                                    start=(c == 0), stop=(c == KC - 1))
            last.then_inc(u_done, 1)
            pe.wait_ge(counts_ready, 1)
            T.matmul(p_att[0:BLOCKS, 0:1], below_n[:], ones[0:PS, 0:1], start=True, stop=True).then_inc(counts_summed, 1)
            pe.wait_ge(start_ready, 1)
            T.matmul(p_att[0:1, 64:64 + BLOCKS], start_col[:], ident[0:BLOCKS, 0:BLOCKS], start=True, stop=True).then_inc(start_turned, 1)
            pe.wait_ge(bn_rows_ready, 1)
            for n in range(4):
                last = T.transpose(p_l3[:, n * R:(n + 1) * R], bn_rows[:, n, :], ident[0:R, 0:R])
            last.then_inc(bn_turned, 1)
            pe.wait_ge(gw_copied, 1)
            pe.wait_ge(starts_ready, 1)
            pe.wait_ge(bn_cols_ready, 1)
            pe.wait_ge(l_small, 48)

            def attention(i, what, q):
                b = i * 2 + q
                if what in ("nt0", "nt1", "nt2"):
                    r = int(what[2])
                    lo, hi = NT_ROUNDS[r]
                    if r == 0:
                        pe.wait_ge(other_ready[q], i + 1)
                        wait(pe, mine_ready, b * 3)
                    if r == 2:
                        pe.wait_ge(mine_ready, b * 3 + 1)
                    for j in range(lo, hi):
                        last = T.transpose(p_nt[r % 2][0:NB, (j - lo) * 128:(j - lo + 1) * 128], other[:, q, :, j], ident_b[:])
                    last.then_inc(nt_done, 1)
                elif what == "colmax":
                    pe.wait_ge(colmax_ready, b + 1)
                    wait(pe, score_ready, b)
                    T.transpose(p_att[0:NB, 0:128], colmax[:], ident[:]).then_inc(colmax_turned, 1)
                elif what == "spread":
                    pe.wait_ge(mine_ready, b * 3 + 3)
                    pe.wait_ge(node_ready, b + 1)
                    for j in range(TILES):
                        last = T.matmul(p_att[:, 128 + 6 * j:134 + 6 * j], mine_T[:, j, :], node6[:], start=True, stop=True)
                    last.then_inc(spread_done, 1)
                elif what.startswith("aggregate"):
                    if what == "aggregate0":
                        pe.wait_ge(wgt_ready, b + 1)
                    for j in range(*AGG_PARTS[int(what[-1])]):
                        last = T.matmul(p_agg[0:NB, 0:F + 1], wgt[:, j, :], rows[:, q, j, 0:F + 1], start=(j == 0), stop=(j == TILES - 1))
                    if what == "aggregate2":
                        last.then_inc(agg_done, 1)
                elif what == "turn":
                    pe.wait_ge(agg_ready, b + 1)
                    if q == 0:
                        wait(pe, base_ready, i)
                    else:
                        pe.wait_ge(x1_ready, b)
                    for c in range(KC):
                        last = T.transpose(p_mix[:, c * NB:(c + 1) * NB], agg[:, c * 128:(c + 1) * 128], ident[0:NB, 0:NB])
                    last.then_inc(agg_turned, 1)
                elif what == "project":
                    pe.wait_ge(aggT_ready, b + 1)
                    for c in range(KC):
                        last = T.matmul(p_mix[0:NB, F:2 * F], aggT[:, c, :], gwT[:, c, :], start=(c == 0), stop=(c == KC - 1))
                    last.then_inc(projected, 1)
                elif what == "turn_x":
                    pe.wait_ge(xn_ready, i + 1)
                    pe.wait_ge(x1_ready, i * 2 + 2)
                    for c in range(KC):
                        for z in range(2):
                            o = (c * 2 + z) * NB
                            last = T.transpose(p_mix[:, o:o + NB], xn[:, z, c * 128:(c + 1) * 128], ident[0:NB, 0:NB])
                    last.then_inc(x_turned, 1)
                elif what == "route":
                    pe.wait_ge(xT_ready, i + 1)
                    for z in range(2):
                        o = p_mix[0:NB, z * EXPERTS:(z + 1) * EXPERTS]
                        for c in range(KC):
                            for part in (HI, LO):
                                T.matmul(o, xT[:, part, c, z * NB:(z + 1) * NB].bitcast(F32), wr[:, c, :],
                                         start=(c == 0 and part == HI), stop=False)
                        last = T.matmul(o, ones[0:1, 0:NB], br_row[:], start=False, stop=True)
                    last.then_inc(routed, 1)
                elif what == "turn_w":
                    pe.wait_ge(r_w_ready, i + 1)
                    for z in range(2):
                        last = T.transpose(p_mix[0:EXPERTS, z * NB:(z + 1) * NB], r_w[:, z, :], ident[0:NB, 0:NB])
                    last.then_inc(w_turned, 1)
                elif what == "bias":
                    pe.wait_ge(wT_ready, i + 1)
                    for z in range(2):
                        last = T.matmul(p_mix[0:NB, z * F:(z + 1) * F], r_wT[:, z * NB:(z + 1) * NB], bo_sb[:], start=True, stop=True)
                    last.then_inc(bias_done, 1)

            def experts(g, layer, e):
                n = g * EXPERTS + e
                if layer == 1:
                    if e == 0:
                        pe.wait_ge(xT_ready, g + 1)
                        pe.wait_ge(w_split, 3 * EXPERTS)
                    pe.wait_ge(h1_ready, n + 1)
                    for m in range(KC):
                        for c in range(KC):
                            for a, b in PRODUCTS:
                                last = T.matmul(p_l1[:, m * 2 * NB:(m + 1) * 2 * NB], w1[:, a, e * KC + c, m * 128:(m + 1) * 128], xT[:, b, c, :],
                                                start=(c == 0 and (a, b) == PRODUCTS[0]), stop=(c == KC - 1 and (a, b) == PRODUCTS[-1]))
                    last.then_inc(l1_done, 1)
                elif layer == 2:
                    pe.wait_ge(h2_ready, n + 1)
                    pe.wait_ge(h1_ready, n + 2)
                    for m in range(KC):
                        for c in range(KC):
                            for a, b in PRODUCTS:
                                last = T.matmul(p_l2[:, m * 2 * NB:(m + 1) * 2 * NB], w2[:, a, e * KC + c, m * 128:(m + 1) * 128], h1[:, e % 2, b, c, :],
                                                start=(c == 0 and (a, b) == PRODUCTS[0]), stop=(c == KC - 1 and (a, b) == PRODUCTS[-1]))
                    last.then_inc(l2_done, 1)
                else:
                    pe.wait_ge(y_added, n + 1)
                    pe.wait_ge(h2_ready, n + 2)
                    for z in range(2):
                        for c in range(KC):
                            for a, b in PRODUCTS:
                                last = T.matmul(p_l3[0:NB, z * F:(z + 1) * F], h2[:, e % 2, a, c, z * NB:(z + 1) * NB], wo[:, b, e * KC + c, :],
                                                start=(c == 0 and (a, b) == PRODUCTS[0]), stop=(c == KC - 1 and (a, b) == PRODUCTS[-1]))
                    last.then_inc(l3_done, 1)

            over_groups(pe, attention, experts)


_INS = ['x', 'src', 'dst', 'edge_attr_64', 'L0_gnn_W', 'L0_gnn_A', 'L0_ffn_Wr', 'L0_ffn_br', 'L0_ffn_W1', 'L0_ffn_b1',
        'L0_ffn_g1', 'L0_ffn_be1', 'L0_ffn_m1', 'L0_ffn_v1', 'L0_ffn_W2', 'L0_ffn_b2', 'L0_ffn_g2', 'L0_ffn_be2',
        'L0_ffn_m2', 'L0_ffn_v2', 'L0_ffn_Wo', 'L0_ffn_bo']


def kernel(**inputs):
    import numpy as _np
    import concourse.bacc as _bacc
    from concourse.bass_utils import run_bass_kernel_spmd as _run

    nc = _bacc.Bacc("TRN2", target_bir_lowering=False, num_devices=1)
    arrays, args = {}, []
    for name in _INS:
        a = _np.ascontiguousarray(inputs[name])
        arrays[f"in_{name}_dram"] = a
        args.append(nc.dram_tensor(f"in_{name}_dram", a.shape, mybir.dt.from_np(a.dtype), kind="ExternalInput").ap())
    out = nc.dram_tensor("out_dram", (NODES, F), F32, kind="ExternalOutput").ap()
    gnn_ffn_program(nc, *args, out)
    r = _run(nc, [arrays], core_ids=[0])
    return _np.asarray(r.results[0]["out_dram"])
```

```python
from contextlib import ExitStack

import concourse.bass as bass
from concourse import mybir

F32 = mybir.dt.float32
F32R = mybir.dt.float32r
BF16 = mybir.dt.bfloat16
I32 = mybir.dt.int32
U32 = mybir.dt.uint32
ALU = mybir.AluOpType
ACT = mybir.ActivationFunctionType
AX = mybir.AxisListType

NODES, EDGES, F, EDIM, EXPERTS = 6250, 100000, 256, 64, 8
NB = 125
NB_HALF = (NB + 1) // 2
BLOCKS = NODES // NB
GROUPS = BLOCKS // 2
TILES = 17
CAP = TILES * 128
ROW = F + 2
KC = F // 128
PIECE = 16
PIECES = EDGES // 125 // PIECE
GENERAL_PHASES = (
    ("begin", 1),
    ("scores", PIECES),
    ("maximum", BLOCKS),
    ("weigh", PIECES),
    ("clear", BLOCKS),
    ("aggregate", PIECES),
    ("finish", BLOCKS),
    ("replace", 1),
)
LIST = NODES + CAP
SPAN = 32
PS = 125
CB = 5
CHUNKS = BLOCKS // CB
CHUNK_BUFS = 4
EVEN_BLOCKS, ODD_BLOCKS = range(0, CB, 2), range(1, CB, 2)
ALPHA, LN_EPS, BN_EPS = 0.2, 1e-5, 1e-3
FAR = 1e30
HI, LO = 0, 1
STAGED = 6
PRODUCTS = ((HI, HI), (HI, LO), (LO, HI))
NT_ROUNDS = [(0, 6), (6, 12), (12, 17)]

SLOTS = 24
FRAMES = 3
BLOCK_STEPS = {
    "edges": 0, "nt0": 1, "scores0": 1, "nt1": 1, "nt2": 3, "scores1": 2, "colmax": 5, "nodemax": 5,
    "spread": 7, "score": 7, "exp": 7, "weights": 8, "aggregate0": 10, "aggregate1": 12, "aggregate2": 12,
    "den": 13, "scale": 13, "turn": 15, "turned": 14, "project": 16, "residual": 16,
}
GROUP_STEPS = {
    "moments": 28, "std": 28, "normalise": 29, "turn_x": 30, "x_hi": 29, "x_lo": 30, "route": 33,
    "route_max": 33, "route_exp": 33, "gates": 34, "turn_w": 35, "turned_w": 37, "bias": 38, "base": 38,
}
AGG_PARTS = [(0, 6), (6, 12), (12, 17)]
BEHIND = {"scalar": 0, "vector": 1}
ATTENTION_FIRST = ()
FIRST_LAYER = {1: 32, 2: 36, 3: 40}


def timetable():
    steps, layers = {}, {}
    for name, slot in BLOCK_STEPS.items():
        for q in range(2):
            steps.setdefault(slot + q * (SLOTS // 2), []).append((name, q))
    for name, slot in GROUP_STEPS.items():
        steps.setdefault(slot, []).append((name, 0))
    for layer, slot in FIRST_LAYER.items():
        for e in range(EXPERTS):
            layers[slot + 3 * e] = (layer, e)
    return steps, layers


STEPS, LAYERS = timetable()


def gnn_ffn_program(nc, x, src, dst, edge_attr, gnn_W, gnn_A, Wr, br, W1, b1, g1, be1, m1, v1,
                    W2, b2, g2, be2, m2, v2, Wo, bo, out):
    table = nc.dram_tensor("table", (NODES, ROW), F32, kind="Internal").ap()
    src_list = nc.dram_tensor("src_list", (EDGES + LIST,), I32, kind="Internal").ap()
    dst_list = nc.dram_tensor("dst_list", (EDGES + LIST,), I32, kind="Internal").ap()
    dst_rows = dst.rearrange("(r s) -> r s", s=SPAN)
    x_blocks = x.rearrange("(b p) f -> p b f", p=NB)
    table_blocks = table.rearrange("(b p) f -> p b f", p=NB)

    with ExitStack() as ctx:
        def sb(name, shape, dt=F32):
            return ctx.enter_context(nc.sbuf_tensor(name, shape, dt))

        def sem(name):
            return ctx.enter_context(nc.semaphore(name))

        def pair(name):
            return [sem(f"{name}{q}") for q in range(2)]

        def bank(name, dt=F32):
            return ctx.enter_context(nc.psum_tensor(name, [128, 2048 // (2 if dt == BF16 else 4)], dt))

        w1 = sb("w1", [128, 2, EXPERTS * KC, F], F32R)
        w2 = sb("w2", [128, 2, EXPERTS * KC, F], F32R)
        wo = sb("wo", [128, 2, EXPERTS * KC, F], F32R)
        gwT = sb("gwT", [128, KC, F])
        a_cols = sb("a_cols", [128, 2 * KC])
        u_cols = sb("u_cols", [128, KC, 2])
        a_e = sb("a_e", [128, EDIM])
        wr = sb("wr", [128, KC, EXPERTS])
        wr_parts = sb("wr_parts", [128, 2, KC, EXPERTS], F32R)
        br_row = sb("br_row", [1, EXPERTS])
        bo_sb = sb("bo_sb", [EXPERTS, F])
        bn_cols = sb("bn_cols", [128, 4, EXPERTS * KC])
        ident = sb("ident", [128, 128])
        ident_b = sb("ident_b", [128, 128], BF16)
        ones = sb("ones", [128, 128])
        eps_ln = sb("eps_ln", [128, 1])
        eps_bn = sb("eps_bn", [128, 1])
        bound_col_i = sb("bound_col_i", [BLOCKS, 1], I32)
        bound_col = sb("bound_col", [BLOCKS, 1])
        row_f = sb("row_f", [BLOCKS, 1])
        row_i = sb("row_i", [BLOCKS, 1], I32)
        in_row_n = sb("in_row_n", [BLOCKS, 1])
        start_col = sb("start_col", [BLOCKS, 1])
        falls = sb("falls", [PS, 1])
        dst_next = sb("dst_next", [PS, 1], I32)
        irregular = sb("irregular", [1, 2])
        irregular_i = sb("irregular_i", [1, 1], I32)
        attr_starts = sb("attr_starts", [1, BLOCKS], I32)
        piece_ids = sb("piece_ids", [PS, PIECE], I32)
        piece_base = sb("piece_base", [PS, 1])
        starts = sb("starts", [1, BLOCKS], I32)
        mv = sb("mv", [NB, 2, CB, 2])
        std = sb("std", [NB, 2, CB])
        rstd = sb("rstd", [NB, 2, CB])
        nmr = sb("nmr", [NB, 2, CB])
        even_dots = sb("even_dots", [NB, 2, len(EVEN_BLOCKS)])
        sdst = sb("sdst", [NB, BLOCKS])
        sdst_r = sb("sdst_r", [NB, BLOCKS])
        sdst3 = sb("sdst3", [NB, BLOCKS, 3], BF16)
        node_ids = sb("node_ids", [128, NB, TILES], BF16)
        block_base = sb("block_base", [128, 2])
        two_blocks = sb("two_blocks", [128, 1])
        dst_l = sb("dst_l", [128, TILES], BF16)
        src_t = sb("src_t", [128, 2, TILES], I32)
        dst_t = sb("dst_t", [128, 2, TILES], I32)
        attr = sb("attr", [128, 2, TILES, EDIM])
        rows = sb("rows", [128, 2, TILES, ROW])
        early = rows.rearrange("p q j f -> p (q j f)")
        TR = CHUNK_BUFS * CB * ROW
        tr = early[0:NB, 0:TR].rearrange("p (q b f) -> p q b f", q=CHUNK_BUFS, b=CB)
        s_edge = sb("s_edge", [128, TILES])
        t_edge = sb("t_edge", [128, 2, TILES])
        other_mem = sb("other_mem", [128, 2 * NB * TILES], BF16)
        other = other_mem.rearrange("p (q n j) -> p q n j", q=2, n=NB)
        masked = sb("masked", [128, NB_HALF, TILES])
        colmax = sb("colmax", [128, NB])
        mine_T = sb("mine_T", [NB, TILES, 128], BF16)
        node_t = sb("node_t", [NB, 4])
        node6 = sb("node6", [NB, 6], BF16)
        spread = sb("spread", [128, TILES, 2])
        logit = sb("logit", [128, TILES])
        score = sb("score", [128, TILES])
        ex = sb("ex", [128, TILES])
        wgt = sb("wgt", [128, TILES, NB])
        den = sb("den", [NB, 2])
        aggT = sb("aggT", [128, KC, NB])
        x1 = sb("x1", [NB, 2, F])
        ln6 = sb("ln6", [NB, 2, 6])
        lnmv = sb("lnmv", [NB, 2, 2])
        lnstd = sb("lnstd", [NB, 2])
        lnr = sb("lnr", [NB, 2])
        xn = sb("xn", [NB, 2, F])
        xT = sb("xT", [128, 2, KC, 2 * NB], F32R)
        r_negmax = sb("r_negmax", [NB, 2])
        r_exp = sb("r_exp", [NB, 2, EXPERTS])
        r_sum = sb("r_sum", [NB, 2])
        r_inv = sb("r_inv", [NB, 2])
        r_w = sb("r_w", [NB, 2, EXPERTS])
        r_wT = aggT.rearrange("p c n -> p (c n)")[0:EXPERTS, :]
        gate = sb("gate", [NB, 2, EXPERTS])
        base = xn
        agg = wgt.rearrange("p j n -> p (j n)")[0:NB, 0:F]
        h1 = sb("h1", [128, 2, 2, KC, 2 * NB], F32R)
        h2 = sb("h2", [128, 2, 2, KC, 2 * NB], F32R)
        h_mem = sb("h_mem", [128, 2, 512])
        h_full = h_mem[:, :, 0:KC * 2 * NB].rearrange("p l (c n) -> p l c n", c=KC)
        acc = sb("acc", [NB, 2, F])

        gw = h_mem[:, 0, :].rearrange("p (c f) -> p c f", c=KC)
        hT = h_mem[:, 1, 0:KC * 2 * NB].rearrange("p (z m) -> p z m", z=2)
        a_wide = other_mem[:, 0:2 * 2 * KC * 128].bitcast(F32).rearrange("p (k n) -> p k n", k=2 * KC)
        u_rows = x1
        junk = other_mem[0:NB, 0:2 * 2 * len(EVEN_BLOCKS) * F].bitcast(F32).rearrange("p (k f) -> p k f", f=F)
        w_staged = early[:, TR:TR + STAGED * KC * F].rearrange("p (n c f) -> p n c f", n=STAGED, c=KC)
        ids_i = early[:, TR:TR + NB * TILES].bitcast(I32)
        R = EXPERTS * KC
        wgt_mem = wgt.rearrange("p j n -> p (j n)")
        bn = wgt_mem[0:R, 0:16 * 128].rearrange("p (k n) -> p k n", n=128)
        bn_in, bn_tmp, bn_rows = bn[:, 0:10], bn[:, 10:12], bn[:, 12:16]
        st6 = wgt_mem[0:NB, 16 * 128:16 * 128 + 12 * CB].rearrange("p (q b k) -> p q b k", q=2, k=6)
        masked_mem = masked.rearrange("p n j -> p (n j)")
        SAMPLES = EDGES // PS // SPAN
        HALF = BLOCKS * SAMPLES // 2
        drops = other_mem[0:PS, 2 * 2 * KC * 128:2 * 2 * KC * 128 + 2 * EDGES // PS].bitcast(F32)
        below = masked_mem[0:PS, 0:HALF].bitcast(BF16).rearrange("p (b n) -> p b n", b=BLOCKS)
        window = masked_mem[0:BLOCKS, HALF:HALF + SPAN].bitcast(I32)
        in_row = masked_mem[0:BLOCKS, HALF + SPAN:HALF + 2 * SPAN]
        dst_all = mine_T.rearrange("p j e -> p (j e)")[0:PS, 0:2 * EDGES // PS].bitcast(I32)

        acc_mem = acc.rearrange("p q f -> p (q f)")
        bound_row, below_n = acc_mem[0:PS, 0:BLOCKS], acc_mem[0:PS, BLOCKS:2 * BLOCKS]
        bound_row_i = acc_mem[0:PS, 2 * BLOCKS:3 * BLOCKS].bitcast(I32)
        first_row, list_row = acc_mem[0:1, 3 * BLOCKS:4 * BLOCKS], acc_mem[0:1, 4 * BLOCKS:5 * BLOCKS]
        start_row = acc_mem[0:1, 5 * BLOCKS:6 * BLOCKS + 1]
        LISTED = NODES // PS + TILES
        node_list = xn[0:PS, 1, 0:2 * LISTED].bitcast(I32).rearrange("p (l n) -> p l n", l=2)
        node_sums = sdst_r
        piece_max = xn[0:PS, 0, 0:NB]
        piece_attr = h_mem.rearrange("p l n -> p (l n)")[0:PS, :].rearrange("p (j d) -> p j d", j=PIECE)
        piece_rows = rows[0:PS, 0, 0:PIECE, :]
        piece_other = other[0:PS, 0, :, 0:PIECE]
        piece_wgt = wgt[0:PS, 0:PIECE, :]
        after_first = NB * TILES + NB * TILES % 2
        edge_values = other_mem[0:PS, after_first:after_first + 2 * (EDGES // PS)].bitcast(F32)
        node_row = acc.rearrange("p q f -> p (q f)")[:, 0:ROW]

        p_agg = bank("p_agg")
        p_nt = [bank("p_nt0", BF16), bank("p_nt1", BF16)]
        p_att = bank("p_att")
        p_mix = bank("p_mix")
        p_l1 = bank("p_l1")
        p_l2 = bank("p_l2")
        p_l3 = bank("p_l3")
        p_dots = [p_l1, p_l2]

        l_gnn = sem("l_gnn")
        l_dst = sem("l_dst")
        l_dst_next = sem("l_dst_next")
        l_bn = sem("l_bn")
        l_small = sem("l_small")
        l_w = sem("l_w")
        wr_split = sem("wr_split")
        w_hi_ready = sem("w_hi_ready")
        w_split = sem("w_split")
        last_hi_ready = sem("last_hi_ready")
        last_split = sem("last_split")
        l_x = [sem(f"l_x{k}") for k in range(CHUNK_BUFS)]
        ident_ready = sem("ident_ready")
        bounds_ready = sem("bounds_ready")
        consts_ready = sem("consts_ready")
        gwT_done = sem("gwT_done")
        a_wide_ready = sem("a_wide_ready")
        u_rows_done = sem("u_rows_done")
        u_copied = sem("u_copied")
        u_done = sem("u_done")
        gw_copied = sem("gw_copied")
        counts_ready = sem("counts_ready")
        counts_summed = sem("counts_summed")
        row_ready = sem("row_ready")
        window_loaded = sem("window_loaded")
        start_ready = sem("start_ready")
        start_turned = sem("start_turned")
        starts_ready = sem("starts_ready")
        lists_ready = sem("lists_ready")
        list_stored = sem("list_stored")
        g_next = sem("g_next")
        g_loaded = sem("g_loaded")
        g_scores_gathered = sem("g_scores_gathered")
        g_maxima_gathered = sem("g_maxima_gathered")
        g_rows_gathered = sem("g_rows_gathered")
        g_sums_loaded = sem("g_sums_loaded")
        g_colmax_ready = sem("g_colmax_ready")
        g_colmax_turned = sem("g_colmax_turned")
        g_block_ready = sem("g_block_ready")
        g_stored = sem("g_stored")
        g_score_ready = sem("g_score_ready")
        g_exp_ready = sem("g_exp_ready")
        g_wgt_ready = sem("g_wgt_ready")
        g_agg_done = sem("g_agg_done")
        g_replaced = sem("g_replaced")
        bn_var_ready = sem("bn_var_ready")
        bn_rows_ready = sem("bn_rows_ready")
        bn_turned = sem("bn_turned")
        bn_cols_ready = sem("bn_cols_ready")
        stats_ready = sem("stats_ready")
        std_ready = sem("std_ready")
        rstd_ready = sem("rstd_ready")
        table_rows = sem("table_rows")
        h_turned = sem("h_turned")
        hT_ready = sem("hT_ready")
        even_dotted = sem("even_dotted")
        dotted = sem("dotted")
        dots_read = sem("dots_read")
        row_complete = sem("row_complete")
        table_stored = pair("table_stored")
        edges_loaded = pair("edges_loaded")
        x_loaded = pair("x_loaded")
        products_ready = pair("products_ready")
        gathered = pair("gathered")
        other_ready = pair("other_ready")
        nt_done = sem("nt_done")
        mine_ready = sem("mine_ready")
        half_ready = sem("half_ready")
        colmax_ready = sem("colmax_ready")
        colmax_turned = sem("colmax_turned")
        node_ready = sem("node_ready")
        spread_done = sem("spread_done")
        score_ready = sem("score_ready")
        exp_ready = sem("exp_ready")
        wgt_ready = sem("wgt_ready")
        agg_done = sem("agg_done")
        den_ready = sem("den_ready")
        agg_ready = sem("agg_ready")
        agg_turned = sem("agg_turned")
        aggT_ready = sem("aggT_ready")
        projected = sem("projected")
        x1_ready = sem("x1_ready")
        moments_ready = sem("moments_ready")
        lnstd_ready = sem("lnstd_ready")
        xn_ready = sem("xn_ready")
        x_turned = sem("x_turned")
        xT_hi_ready = sem("xT_hi_ready")
        xT_ready = sem("xT_ready")
        routed = sem("routed")
        negmax_ready = sem("negmax_ready")
        r_exp_ready = sem("r_exp_ready")
        r_w_ready = sem("r_w_ready")
        w_turned = sem("w_turned")
        wT_ready = sem("wT_ready")
        bias_done = sem("bias_done")
        base_ready = sem("base_ready")
        l1_done = sem("l1_done")
        h1_full = sem("h1_full")
        h1_hi_ready = sem("h1_hi_ready")
        h1_ready = sem("h1_ready")
        l2_done = sem("l2_done")
        h2_full = sem("h2_full")
        h2_hi_ready = sem("h2_hi_ready")
        h2_ready = sem("h2_ready")
        l3_done = sem("l3_done")
        y_added = sem("y_added")
        out_stored = sem("out_stored")

        def wait(eng, semaphore, value):
            if not isinstance(value, int) or value > 0:
                eng.wait_ge(semaphore, value)

        def staged_weights(r, n):
            k = (2 * r + n // 3) * KC
            return (w1, w2, wo)[n % 3][:, :, k:k + KC]

        def take(eng, semaphore, value):
            eng.wait_ge(semaphore, value)
            eng.sem_clear(semaphore)

        def general_path(eng, **parts):
            eng.wait_ge(starts_ready, 1)
            found = eng.value_load(irregular_i[0:1, 0:1], min_val=0, max_val=1)
            with eng.If(found > 0):
                for phase, count in GENERAL_PHASES:
                    if phase in parts and count == 1:
                        parts[phase]()
                    elif phase in parts:
                        with eng.Fori(0, count) as k:
                            parts[phase](k)

        def over_groups(eng, attention, experts, behind=0, attention_first=False):
            def frame(i, ages):
                for s in range(SLOTS):
                    for part in ("attention", "experts") if attention_first else ("experts", "attention"):
                        for age in ages:
                            slot = s + age * SLOTS
                            if part == "experts" and slot - behind in LAYERS:
                                experts(i - age, *LAYERS[slot - behind])
                            if part == "attention":
                                for what, q in STEPS.get(slot, []):
                                    attention(i - age, what, q)
            frame(0, (0,))
            frame(1, (1, 0))
            with eng.Fori(FRAMES - 1, GROUPS) as i:
                frame(i, (2, 1, 0))
            frame(GROUPS, (2, 1))
            frame(GROUPS + 1, (2,))

        block = ctx.enter_context(nc.Block())

        @block.sync
        def _(sp):
            sp.dma_start(gw, gnn_W.rearrange("(c p) f -> p c f", p=128)).then_inc(l_gnn, 16)
            sp.dma_start(a_cols[:], gnn_A[0, 0:2 * F].rearrange("(c p) -> p c", p=128), allow_slow_non_contiguous=True).then_inc(l_gnn, 16)
            sp.dma_start(a_e[:], gnn_A[0:1, 2 * F:2 * F + EDIM].broadcast_to([128, EDIM])).then_inc(l_gnn, 16)

            def load_chunk(c):
                sp.dma_start(tr[:, c % CHUNK_BUFS, :, 0:F], x_blocks[:, c * CB:(c + 1) * CB, :]).then_inc(l_x[c % CHUNK_BUFS], 16)

            load_chunk(0)
            sp.dma_start(dst_all, dst.rearrange("(p n) -> p n", p=PS)).then_inc(l_dst, 16)
            load_chunk(1)
            load_chunk(2)
            load_chunk(3)
            sp.wait_ge(ident_ready, 1)
            sp.dma_start(dst_next[0:PS - 1, :], dst.rearrange("(p n) -> p n", p=PS)[1:PS, 0:1], allow_slow_non_contiguous=True).then_inc(l_dst_next, 16)
            sp.dma_start(src_list[0:EDGES], src).then_inc(list_stored, 16)
            sp.dma_start(dst_list[0:EDGES], dst).then_inc(list_stored, 16)
            sp.wait_ge(lists_ready, 1)
            C = NODES // PS
            for l, of in enumerate((src_list, dst_list)):
                sp.dma_start(of[EDGES:EDGES + NODES].rearrange("(p n) -> p n", p=PS), node_list[:, l, 0:C]).then_inc(list_stored, 16)
                sp.dma_start(of[EDGES + NODES:EDGES + NODES + PS * TILES].rearrange("(p n) -> p n", p=PS), node_list[:, l, C:C + TILES]).then_inc(list_stored, 16)
            for n, a in enumerate((b1, g1, be1, m1, v1, b2, g2, be2, m2, v2)):
                sp.dma_start(bn_in[:, n, :], a.rearrange("e (c p) -> (e c) p", p=128)).then_inc(l_bn, 16)
            sp.dma_start(wr[:], Wr.rearrange("(c p) e -> p c e", p=128)).then_inc(l_small, 16)
            sp.dma_start(br_row[:], br.rearrange("(o e) -> o e", o=1)).then_inc(l_small, 16)
            sp.dma_start(bo_sb[:], bo).then_inc(l_small, 16)

            sp.wait_ge(consts_ready, 1)

            def stage_weights(r):
                for n in range(STAGED):
                    w, k = (W1, W2, Wo)[n % 3], n // 3
                    sp.dma_start(w_staged[:, n], w[r * 2 + k].rearrange("(c p) f -> p c f", p=128)).then_inc(l_w, 16)

            def load_edges(i, q):
                first = sp.value_load(starts[0:1, bass.ds(i * 2 + q, 1)], min_val=0, max_val=EDGES + LIST - CAP)
                first_attr = sp.value_load(attr_starts[0:1, bass.ds(i * 2 + q, 1)], min_val=0, max_val=EDGES - CAP)
                for t, of in ((src_t, src_list), (dst_t, dst_list)):
                    sp.dma_start(t[:, q, :], of[bass.ds(first, CAP)].rearrange("(p j) -> p j", j=TILES)).then_inc(edges_loaded[q], 16)
                sp.dma_start(attr[:, q], edge_attr[bass.ds(first_attr, CAP), :].rearrange("(p j) d -> p j d", j=TILES)).then_inc(edges_loaded[q], 16)

            def load_x(i, q):
                sp.dma_start(x1[:, q, :], x[bass.ds(i * (2 * NB) + q * NB, NB), :]).then_inc(x_loaded[q], 16)

            def store_out(g):
                sp.wait_ge(y_added, g * EXPERTS + EXPERTS + 1)
                sp.dma_start(out[bass.ds(g * (2 * NB), 2 * NB), :].rearrange("(q p) f -> p q f", p=NB), acc[:]).then_inc(out_stored, 16)

            def next_edges(i):
                for q in range(2):
                    sp.wait_ge(gathered[q], i * (16 * TILES))
                    sp.wait_ge(other_ready[q], i)
                    load_edges(i, q)

            def next_x(i):
                sp.wait_ge(base_ready, i)
                for q in range(2):
                    load_x(i, q)

            for c in range(CHUNKS):
                if CHUNK_BUFS <= c + 3 < CHUNKS:
                    sp.wait_ge(table_stored[(c - 1) % 2], (c + 1) // 2 * 16)
                    load_chunk(c + 3)
                if c == 0:
                    stage_weights(0)
                if c == 4:
                    sp.wait_ge(w_split, STAGED)
                    stage_weights(1)
                if c == CHUNKS - 2:
                    sp.wait_ge(starts_ready, 1)
                    sp.wait_ge(list_stored, 6 * 16)
                    load_edges(0, 0)
                sp.wait_ge(row_complete, c + 1)
                sp.dma_start(table_blocks[:, c * CB:(c + 1) * CB, :], tr[:, c % CHUNK_BUFS]).then_inc(table_stored[c % 2], 16)
            load_edges(0, 1)
            sp.wait_ge(w_split, 2 * STAGED)
            stage_weights(2)

            src_pieces = src.rearrange("(p n) -> p n", p=PS)
            dst_pieces = dst.rearrange("(p n) -> p n", p=PS)
            attr_pieces = edge_attr.rearrange("(p n) d -> p n d", p=PS)

            def load_scores(w):
                take(sp, g_next, 1)
                sp.dma_start(piece_ids[:], src_pieces[:, bass.ds(w * PIECE, PIECE)]).then_inc(g_loaded, 16)
                sp.dma_start(piece_attr, attr_pieces[:, bass.ds(w * PIECE, PIECE), :]).then_inc(g_loaded, 16)

            def store_block(b):
                take(sp, g_block_ready, 1)
                sp.dma_start(out[bass.ds(b * NB, NB), :], node_row[:, 0:F]).then_inc(g_stored, 16)

            def load_targets(w):
                take(sp, g_next, 1)
                sp.dma_start(piece_ids[:], dst_pieces[:, bass.ds(w * PIECE, PIECE)]).then_inc(g_loaded, 16)

            def update_block(b):
                take(sp, g_next, 1)
                sp.dma_start(node_row[:, 0:F], out[bass.ds(b * NB, NB), :]).then_inc(g_sums_loaded, 16)
                store_block(b)

            def load_sources(w):
                take(sp, g_next, 1)
                sp.dma_start(piece_ids[:], src_pieces[:, bass.ds(w * PIECE, PIECE)]).then_inc(g_loaded, 16)
                with sp.Fori(0, BLOCKS) as b:
                    update_block(b)

            def replace_rows():
                take(sp, g_next, 1)
                sp.dma_start(table[:, 0:F], out).then_inc(g_replaced, 16)

            general_path(sp, scores=load_scores, maximum=store_block, weigh=load_targets, clear=store_block,
                         aggregate=load_sources, finish=update_block, replace=replace_rows)
            sp.wait_ge(last_split, STAGED)
            stage_weights(3)
            for q in range(2):
                load_x(0, q)
            next_edges(1)
            next_edges(2)
            next_x(1)
            with sp.Fori(2, GROUPS - 1) as i:
                next_edges(i + 1)
                next_x(i)
                store_out(i - 2)
            next_x(GROUPS - 1)
            for g in range(GROUPS - 3, GROUPS):
                store_out(g)
            sp.wait_ge(out_stored, 16 * (GROUPS + 1))

        @block.gpsimd
        def _(pool):
            nc.gpsimd.memset(ident[:], 0.0)
            nc.gpsimd.memset(eps_ln[:], LN_EPS)
            nc.gpsimd.memset(dst_next[:], NODES)
            nc.gpsimd.memset(eps_bn[:], BN_EPS)
            pool.drain()
            nc.gpsimd.affine_select(out=ident[:], in_=ident[:], compare_op=ALU.not_equal, fill=1.0, base=0,
                                    pattern=[[-1, 128]], channel_multiplier=1).then_inc(ident_ready, 1)
            nc.gpsimd.memset(ones[:], 1.0)
            nc.gpsimd.iota(bound_row_i, pattern=[[NB, BLOCKS]], base=0, channel_multiplier=0)
            nc.gpsimd.iota(bound_col_i[:], pattern=[[0, 1]], base=0, channel_multiplier=NB)
            nc.gpsimd.memset(two_blocks[:], float(2 * NB))
            for q in range(2):
                nc.gpsimd.memset(block_base[:, q:q + 1], float(NB * q - 2 * NB))
            pool.drain()
            nc.gpsimd.tensor_copy(bound_row, bound_row_i)
            nc.gpsimd.tensor_copy(bound_col[:], bound_col_i[:]).then_inc(bounds_ready, 1)
            C = NODES // PS
            nc.gpsimd.iota(node_list[:, 0, 0:C], pattern=[[1, C]], base=0, channel_multiplier=C)
            nc.gpsimd.iota(node_list[:, 0, C:C + TILES], pattern=[[1, TILES]], base=0, channel_multiplier=TILES)
            nc.gpsimd.iota(node_list[:, 1, 0:C], pattern=[[1, C]], base=0, channel_multiplier=C)
            nc.gpsimd.iota(node_list[:, 1, C:C + TILES], pattern=[[1, TILES]], base=NODES, channel_multiplier=TILES).then_inc(lists_ready, 1)
            nc.gpsimd.iota(ids_i, pattern=[[1, NB], [0, TILES]], base=0, channel_multiplier=0)
            pool.drain()
            nc.gpsimd.tensor_copy(ident_b[:], ident[:])
            nc.gpsimd.tensor_copy(node_ids.rearrange("p n j -> p (n j)"), ids_i).then_inc(consts_ready, 1)

            def split_weights(i):
                for n in range(STAGED):
                    pool.wait_ge(l_w, i * (16 * STAGED) + 16 * STAGED)
                    w, k = (w1, w2, wo)[n % 3], n // 3
                    e = bass.ds(i * (2 * KC) + k * KC, KC)
                    nc.gpsimd.tensor_copy(w[:, HI, e], w_staged[:, n]).then_inc(w_hi_ready, 1)
                    pool.wait_ge(w_hi_ready, i * STAGED + n + 1)
                    nc.gpsimd.tensor_tensor(w[:, LO, e], w_staged[:, n], w[:, HI, e].bitcast(F32), ALU.subtract).then_inc(w_split, 1)

            pool.wait_ge(row_ready, 1)
            nc.gpsimd.indirect_dma_start(window, None, dst_rows, bass.IndirectOffsetOnAxis(ap=row_i[:].bitcast(U32), axis=0)).then_inc(window_loaded, 16)
            with pool.Fori(0, EXPERTS // 2 - 2) as i:
                split_weights(i)
            for parity in range(2):
                pool.wait_ge(table_stored[parity], 16 * (CHUNKS // 2))

            def gather_piece(into, of, loads, gathered_):
                take(pool, g_loaded, 16 * loads)
                for j in range(PIECE):
                    nc.gpsimd.indirect_dma_start(into[:, j, :], None, of,
                                                 bass.IndirectOffsetOnAxis(ap=piece_ids[:, j:j + 1].bitcast(U32), axis=0)).then_inc(gathered_, 16)

            general_path(pool, scores=lambda w: gather_piece(piece_rows, table, 2, g_scores_gathered),
                         weigh=lambda w: gather_piece(piece_rows[:, :, 0:F], out, 1, g_maxima_gathered),
                         aggregate=lambda w: gather_piece(piece_rows, table, 1, g_rows_gathered),
                         replace=lambda: take(pool, g_replaced, 16))

            def gather(i, q):
                wait(pool, other_ready[q], i)
                pool.wait_ge(edges_loaded[q], i * 48 + 48)
                nc.gpsimd.tensor_tensor(block_base[:, q:q + 1], block_base[:, q:q + 1], two_blocks[:], ALU.add)
                wait(pool, agg_done, i * 2 + q - 1)
                nc.gpsimd.tensor_tensor(attr[:, q], attr[:, q], a_e[:].unsqueeze(1).broadcast_to([128, TILES, EDIM]),
                                        ALU.mult).then_inc(products_ready[q], 1)
                for j in range(TILES):
                    nc.gpsimd.indirect_dma_start(
                        rows[:, q, j, :], None, table,
                        bass.IndirectOffsetOnAxis(ap=src_t[:, q, j:j + 1].bitcast(U32), axis=0)).then_inc(gathered[q], 16)

            gather(0, 0)
            pool.wait_ge(last_split, 2 * STAGED)
            gather(0, 1)
            with pool.Fori(1, GROUPS) as i:
                for q in range(2):
                    gather(i, q)

        @block.scalar
        def _(act):
            act.nop().then_inc(h1_ready, 1)
            act.nop().then_inc(h2_ready, 1)
            act.nop().then_inc(out_stored, 16)
            act.wait_ge(ident_ready, 1)
            def deviations(c, k):
                act.wait_ge(stats_ready, c + 1)
                nc.scalar.activation(std[:, k % 2, :], mv[:, k % 2, :, 1], ACT.Sqrt, bias=eps_ln[0:NB, :]).then_inc(std_ready, 1)

            def normalise_rows(c, k, blocks):
                for b in blocks:
                    nc.scalar.activation(tr[:, k, b, 0:F], tr[:, k, b, 0:F], ACT.Identity,
                                         bias=nmr[:, k % 2, b:b + 1], scale=rstd[:, k % 2, b:b + 1]).then_inc(table_rows, 1)

            def over_chunks(c, k):
                for n, b in enumerate(ODD_BLOCKS):
                    act.wait_ge(h_turned, c * len(ODD_BLOCKS) + n + 1)
                    act.wait_ge(dotted, c * len(ODD_BLOCKS) + n + 1)
                    nc.scalar.activation(hT[:, n], (p_mix, p_agg)[n][:, 0:KC * NB], ACT.Copy).then_inc(hT_ready, 1)
                    if not isinstance(c, int) or c + 1 < CHUNKS:
                        if n == 0:
                            act.wait_ge(rstd_ready, c + 2)
                        normalise_rows(c + 1, (k + 1) % CHUNK_BUFS, (range(0, 3), range(3, CB))[n])
                if not isinstance(c, int) or c + 2 < CHUNKS:
                    deviations(c + 2, (k + 2) % CHUNK_BUFS)

            deviations(0, 0)
            act.wait_ge(rstd_ready, 1)
            normalise_rows(0, 0, range(CB))
            deviations(1, 1)
            with act.Fori(0, CHUNKS // CHUNK_BUFS) as i:
                for k in range(CHUNK_BUFS):
                    over_chunks(i * CHUNK_BUFS + k, k)
            for c in range(CHUNKS // CHUNK_BUFS * CHUNK_BUFS, CHUNKS):
                over_chunks(c, c % CHUNK_BUFS)

            def attention(i, what, q):
                b = i * 2 + q
                if what in ("nt0", "nt1", "nt2"):
                    r = int(what[2])
                    lo, hi = NT_ROUNDS[r]
                    act.wait_ge(nt_done, b * 3 + r + 1)
                    if r == 0:
                        wait(act, spread_done, b)
                    nc.scalar.activation(mine_T[:, lo:hi, :].rearrange("p j e -> p (j e)"),
                                         p_nt[(r) % 2][0:NB, 0:(hi - lo) * 128], ACT.Copy, bias=1.0, scale=-1.0).then_inc(mine_ready, 1)
                elif what == "exp":
                    act.wait_ge(score_ready, b + 1)
                    wait(act, wgt_ready, b)
                    nc.scalar.activation(ex[:], score[:], ACT.Exp).then_inc(exp_ready, 1)
                elif what == "scale":
                    act.wait_ge(den_ready, b + 1)
                    wait(act, agg_turned, b)
                    nc.scalar.activation(agg, p_agg[0:NB, 0:F], ACT.Copy, scale=den[:, 1:2]).then_inc(agg_ready, 1)
                elif what == "turned":
                    act.wait_ge(agg_turned, b + 1)
                    nc.scalar.activation(aggT.rearrange("p c n -> p (c n)"), p_mix[:, 0:KC * NB], ACT.Copy).then_inc(aggT_ready, 1)
                elif what == "std":
                    act.wait_ge(moments_ready, i + 1)
                    nc.scalar.activation(lnstd[:], lnmv[:, :, 1], ACT.Sqrt, bias=eps_ln[0:NB, :]).then_inc(lnstd_ready, 1)
                elif what == "x_hi":
                    act.wait_ge(x_turned, i + 1)
                    nc.scalar.activation(xT[:, HI].rearrange("p c n -> p (c n)"), p_mix[:, 0:KC * 2 * NB], ACT.Copy).then_inc(xT_hi_ready, 1)
                elif what == "route_exp":
                    act.wait_ge(negmax_ready, i + 1)
                    for z in range(2):
                        last = nc.scalar.activation(r_exp[:, z, :], p_mix[0:NB, z * EXPERTS:(z + 1) * EXPERTS], ACT.Exp,
                                                    bias=r_negmax[:, z:z + 1], accum_out=r_sum[:, z:z + 1])
                    last.then_inc(r_exp_ready, 1)
                elif what == "turned_w":
                    act.wait_ge(w_turned, i + 1)
                    nc.scalar.activation(r_wT, p_mix[0:EXPERTS, 0:2 * NB], ACT.Copy).then_inc(wT_ready, 1)

            def experts(g, layer, e):
                n = g * EXPERTS + e
                if layer == 3:
                    return
                done, bank_, h, full, hi_ready, lo_ready = ((l1_done, p_l1, h1, h1_full, h1_hi_ready, h1_ready),
                                                            (l2_done, p_l2, h2, h2_full, h2_hi_ready, h2_ready))[layer - 1]
                act.wait_ge(lo_ready, n + 1)
                act.wait_ge(done, n + 1)
                for m in range(KC):
                    k = e * KC + m
                    last = nc.scalar.activation(h_full[:, layer - 1, m, :], bank_[:, m * 2 * NB:(m + 1) * 2 * NB], ACT.Relu,
                                                bias=bn_cols[:, 2 * layer - 1, k:k + 1], scale=bn_cols[:, 2 * layer - 2, k:k + 1])
                last.then_inc(full, 1)
                act.wait_ge(full, n + 1)
                nc.scalar.activation(h[:, e % 2, HI], h_full[:, layer - 1], ACT.Copy).then_inc(hi_ready, 1)

            act.wait_ge(l_bn, 160)
            for l in range(2):
                last = nc.scalar.activation(bn_tmp[:, l, :], bn_in[:, 5 * l + 4, :], ACT.Sqrt, bias=eps_bn[0:EXPERTS * KC, :])
            last.then_inc(bn_var_ready, 1)

            def exp_piece(w):
                take(act, g_score_ready, 1)
                nc.scalar.activation(ex[0:PS, 0:PIECE], score[0:PS, 0:PIECE], ACT.Exp).then_inc(g_exp_ready, 1)

            general_path(act, weigh=exp_piece)

            for r in (2, 3):
                act.wait_ge(l_w, 16 * STAGED * (r + 1))
                for n in range(STAGED):
                    nc.scalar.activation(staged_weights(r, n)[:, HI], w_staged[:, n], ACT.Copy).then_inc(last_hi_ready, 1)
            act.wait_ge(bn_cols_ready, 1)
            over_groups(act, attention, experts, BEHIND["scalar"], "scalar" in ATTENTION_FIRST)

        @block.vector
        def _(v):
            V = nc.vector
            v.nop().then_inc(y_added, 1)
            V.memset(tr[:, :, :, F:F + 1], 1.0)
            v.wait_ge(l_gnn, 48)
            V.tensor_copy(a_wide, a_cols[:].unsqueeze(2).broadcast_to([128, 2 * KC, 128])).then_inc(a_wide_ready, 1)
            V.memset(start_row[:, BLOCKS:BLOCKS + 1], float(EDGES))

            def stats(c, k):
                v.wait_ge(l_x[k], (c - k) * (16 // CHUNK_BUFS) + 16)
                for b in range(CB):
                    V.bn_stats(st6[:, k % 2, b, :], tr[:, k, b, 0:F])
                v.drain()
                for b in range(CB):
                    last = V.bn_aggr(mv[:, k % 2, b, :], st6[:, k % 2, b, :])
                last.then_inc(stats_ready, 1)

            def scale(c, k):
                v.wait_ge(std_ready, c + 1)
                V.reciprocal(rstd[:, k % 2, :], std[:, k % 2, :])
                v.drain()
                V.scalar_tensor_tensor(out=nmr[:, k % 2, :], in0=mv[:, k % 2, :, 0], scalar=-1.0, in1=rstd[:, k % 2, :],
                                       op0=ALU.mult, op1=ALU.mult).then_inc(rstd_ready, 1)

            def complete_rows(c, k):
                v.wait_ge(even_dotted, c + 1)
                for n, at in enumerate((tr[:, k, :, F + 1], sdst[:, bass.ds(c * CB, CB)])):
                    last = V.tensor_copy(at[:, 0:CB:2], even_dots[:, n, :])
                v.wait_ge(dotted, c * len(ODD_BLOCKS) + len(ODD_BLOCKS) + 2)
                dots = p_dots[k % 2][0:NB, 0:2 * len(ODD_BLOCKS)].rearrange("p (b s) -> p b s", s=2)
                V.tensor_copy(tr[:, k, 1:CB:2, F + 1], dots[:, :, 0]).then_inc(row_complete, 1)
                V.tensor_copy(sdst[:, bass.ds(c * CB, CB)][:, 1:CB:2], dots[:, :, 1]).then_inc(dots_read, 1)

            def over_chunks(c, k):
                more = not isinstance(c, int) or c + 2 < CHUNKS
                if more:
                    stats(c + 2, (k + 2) % CHUNK_BUFS)
                else:
                    v.drain()
                for m, b in enumerate(EVEN_BLOCKS):
                    v.wait_ge(table_rows, c * CB + b + 1)
                    for n in range(2):
                        last = V.tensor_tensor_reduce(junk[:, 2 * m + n, :], tr[:, k, b, 0:F], u_rows[:, n, :], 1.0, 0.0, ALU.mult, ALU.add,
                                                      even_dots[:, n, m:m + 1])
                last.then_inc(even_dotted, 1)
                complete_rows(c, k)
                if more:
                    scale(c + 2, (k + 2) % CHUNK_BUFS)

            def count_samples():
                v.wait_ge(l_dst, 16)
                v.wait_ge(bounds_ready, 1)
                V.tensor_tensor(below, dst_all.rearrange("p (n s) -> p n s", s=SPAN)[:, :, 0].unsqueeze(1).broadcast_to([PS, BLOCKS, SAMPLES]),
                                bound_row[0:PS, :].unsqueeze(2).broadcast_to([PS, BLOCKS, SAMPLES]), ALU.is_lt)
                v.drain()
                V.tensor_reduce(below_n, below, AX.X, ALU.add).then_inc(counts_ready, 1)

            def count_falls():
                v.wait_ge(l_dst_next, 16)
                V.tensor_tensor(drops[:, 0:EDGES // PS - 1], dst_all[:, 0:EDGES // PS - 1], dst_all[:, 1:EDGES // PS], ALU.is_gt)
                V.tensor_tensor(drops[:, EDGES // PS - 1:], dst_all[:, EDGES // PS - 1:], dst_next[:], ALU.is_gt)
                v.drain()
                V.tensor_reduce(falls[:], drops, AX.X, ALU.add)

            def find_rows():
                v.wait_ge(counts_summed, 1)
                V.tensor_scalar(row_f[:], p_att[0:BLOCKS, 0:1], -1.0, 0.0, ALU.add, ALU.max)
                v.drain()
                V.tensor_copy(row_i[:], row_f[:]).then_inc(row_ready, 1)

            def find_starts():
                v.wait_ge(window_loaded, 16)
                V.tensor_scalar(in_row, window, bound_col[:, 0:1], None, ALU.is_lt)
                v.drain()
                V.tensor_reduce(in_row_n[:], in_row, AX.X, ALU.add)
                v.drain()
                start_col_made = V.scalar_tensor_tensor(out=start_col[:], in0=row_f[:], scalar=float(SPAN), in1=in_row_n[:], op0=ALU.mult, op1=ALU.add)
                start_col_made.then_inc(start_ready, 1)

            def find_windows():
                v.wait_ge(start_turned, 1)
                V.tensor_copy(start_row[:, 0:BLOCKS], p_att[0:1, 64:64 + BLOCKS])
                v.drain()
                V.tensor_scalar(first_row, start_row[:, 0:BLOCKS], float(EDGES - CAP), None, ALU.min)
                v.drain()
                V.tensor_tensor(list_row, start_row[:, 1:BLOCKS + 1], first_row, ALU.subtract)
                v.drain()
                V.tensor_reduce(irregular[:, 0:1], list_row, AX.X, ALU.max)
                v.drain()
                V.tensor_scalar(irregular[:, 0:1], irregular[:, 0:1], float(CAP), None, ALU.is_gt)
                V.tensor_scalar(irregular[:, 1:2], p_att[0:1, 120:121], 0.0, None, ALU.is_gt)
                v.drain()
                V.tensor_tensor(irregular[:, 0:1], irregular[:, 0:1], irregular[:, 1:2], ALU.max)
                V.scalar_tensor_tensor(out=list_row, in0=bound_row[0:1, :], scalar=float(EDGES), in1=first_row, op0=ALU.add, op1=ALU.subtract)
                v.drain()
                V.scalar_tensor_tensor(out=list_row, in0=list_row, scalar=irregular[:, 0:1], in1=first_row, op0=ALU.mult, op1=ALU.add)
                V.tensor_copy(irregular_i[:], irregular[:, 0:1])
                V.tensor_copy(attr_starts[:], first_row)
                v.drain()
                V.tensor_copy(starts[:], list_row).then_inc(starts_ready, 1)

            stats(0, 0)
            v.wait_ge(gwT_done, 1)
            V.tensor_copy(gwT.rearrange("p c f -> p (c f)"), p_l1[:, :]).then_inc(gw_copied, 1)
            count_samples()
            v.wait_ge(u_done, 1)
            V.tensor_copy(u_cols.rearrange("p c s -> p (c s)"), p_l2[:, 0:2 * KC])
            v.wait_ge(u_rows_done, 1)
            V.tensor_copy(u_rows.rearrange("p s f -> p (s f)"), p_l3[0:NB, :]).then_inc(u_copied, 1)
            find_rows()
            scale(0, 0)
            stats(1, 1)
            scale(1, 1)
            count_falls()
            find_starts()
            find_windows()
            with v.Fori(0, CHUNKS // CHUNK_BUFS) as i:
                for k in range(CHUNK_BUFS):
                    over_chunks(i * CHUNK_BUFS + k, k)
            for c in range(CHUNKS // CHUNK_BUFS * CHUNK_BUFS, CHUNKS):
                over_chunks(c, c % CHUNK_BUFS)
            v.wait_ge(bn_var_ready, 1)
            V.reciprocal(bn_tmp, bn_tmp)
            v.drain()
            for l in range(2):
                V.tensor_tensor(bn_rows[:, 2 * l, :], bn_in[:, 5 * l + 1, :], bn_tmp[:, l, :], ALU.mult)
                V.tensor_tensor(bn_rows[:, 2 * l + 1, :], bn_in[:, 5 * l, :], bn_in[:, 5 * l + 3, :], ALU.subtract)
                v.drain()
                V.tensor_tensor(bn_rows[:, 2 * l + 1, :], bn_rows[:, 2 * l + 1, :], bn_rows[:, 2 * l, :], ALU.mult)
                v.drain()
                last = V.tensor_tensor(bn_rows[:, 2 * l + 1, :], bn_rows[:, 2 * l + 1, :], bn_in[:, 5 * l + 2, :], ALU.add)
            last.then_inc(bn_rows_ready, 1)
            v.wait_ge(bn_turned, 1)
            V.tensor_copy(bn_cols.rearrange("p n k -> p (n k)"), p_l3[:, 0:4 * EXPERTS * KC]).then_inc(bn_cols_ready, 1)
            v.drain()
            V.tensor_copy(sdst3[:, :, 0], sdst[:])
            v.drain()
            V.tensor_tensor(sdst_r[:], sdst[:], sdst3[:, :, 0], ALU.subtract)
            v.drain()
            V.tensor_copy(sdst3[:, :, 1], sdst_r[:])
            v.drain()
            V.tensor_tensor(sdst_r[:], sdst_r[:], sdst3[:, :, 1], ALU.subtract)
            v.drain()
            V.tensor_copy(sdst3[:, :, 2], sdst_r[:])
            v.drain()

            def scores_piece(w):
                v.wait_ge(g_scores_gathered, w * (16 * PIECE) + 16 * PIECE)
                V.tensor_tensor(piece_attr, piece_attr, a_e[0:PS].unsqueeze(1).broadcast_to([PS, PIECE, EDIM]), ALU.mult)
                v.drain()
                V.tensor_reduce(s_edge[0:PS, 0:PIECE], piece_attr, AX.X, ALU.add)
                v.drain()
                V.tensor_tensor(edge_values[:, bass.ds(w * PIECE, PIECE)], piece_rows[:, :, F + 1], s_edge[0:PS, 0:PIECE], ALU.add)
                v.drain()
                v.nop().then_inc(g_next, 1)

            def others(w):
                V.tensor_scalar(dst_l[0:PS, 0:PIECE], dst_all[:, bass.ds(w * PIECE, PIECE)], piece_base[:], None, ALU.subtract)
                v.drain()
                V.tensor_tensor(piece_other, dst_l[0:PS, 0:PIECE].unsqueeze(1).broadcast_to([PS, NB, PIECE]),
                                node_ids[0:PS, :, 0:PIECE], ALU.not_equal)
                v.drain()

            def hand_block():
                v.drain()
                v.nop().then_inc(g_block_ready, 1)
                take(v, g_stored, 16)

            def maximum(b):
                V.memset(colmax[:], -2 * FAR)
                v.drain()
                with v.Fori(0, PIECES) as w:
                    others(w)
                    for lo, hi in ((0, NB_HALF), (NB_HALF, NB)):
                        part = masked[0:PS, 0:hi - lo, 0:PIECE]
                        V.scalar_tensor_tensor(out=part, in0=piece_other[:, lo:hi], scalar=-FAR,
                                               in1=edge_values[:, bass.ds(w * PIECE, PIECE)].unsqueeze(1).broadcast_to([PS, hi - lo, PIECE]),
                                               op0=ALU.mult, op1=ALU.add)
                        v.drain()
                        V.tensor_reduce(piece_max[:, lo:hi], part, AX.X, ALU.max)
                        v.drain()
                    V.tensor_tensor(colmax[0:PS], colmax[0:PS], piece_max, ALU.max)
                    v.drain()
                v.nop().then_inc(g_colmax_ready, 1)
                take(v, g_colmax_turned, 1)
                V.tensor_reduce(node_t[:, 0:1], p_att[0:NB, 0:128], AX.X, ALU.max)
                v.drain()
                V.tensor_copy(node_row[:, 0:1], sdst[:, bass.ds(b, 1)])
                v.drain()
                V.tensor_tensor(node_t[:, 1:2], node_t[:, 0:1], node_row[:, 0:1], ALU.add)
                v.drain()
                V.scalar_tensor_tensor(out=node_row[:, 1:2], in0=node_t[:, 1:2], scalar=ALPHA, in1=node_t[:, 1:2],
                                       op0=ALU.mult, op1=ALU.max)
                V.tensor_scalar(piece_base[:], piece_base[:], float(NB), None, ALU.add)
                v.drain()
                hand_block()

            def weigh(w):
                v.wait_ge(g_maxima_gathered, w * (16 * PIECE) + 16 * PIECE)
                values = edge_values[:, bass.ds(w * PIECE, PIECE)]
                V.tensor_tensor(logit[0:PS, 0:PIECE], values, piece_rows[:, :, 0], ALU.add)
                v.drain()
                V.scalar_tensor_tensor(out=score[0:PS, 0:PIECE], in0=logit[0:PS, 0:PIECE], scalar=ALPHA, in1=logit[0:PS, 0:PIECE],
                                       op0=ALU.mult, op1=ALU.max)
                v.drain()
                V.tensor_tensor(logit[0:PS, 0:PIECE], score[0:PS, 0:PIECE], piece_rows[:, :, 1], ALU.subtract)
                v.drain()
                V.tensor_scalar(score[0:PS, 0:PIECE], logit[0:PS, 0:PIECE], 0.0, None, ALU.min).then_inc(g_score_ready, 1)
                take(v, g_exp_ready, 1)
                V.tensor_copy(values, ex[0:PS, 0:PIECE])
                v.drain()
                v.nop().then_inc(g_next, 1)

            def clear(b):
                V.memset(node_row, 0.0)
                hand_block()

            def aggregate_piece(w):
                v.wait_ge(g_rows_gathered, w * (16 * PIECE) + 16 * PIECE)
                V.tensor_scalar(piece_base[:], piece_base[:], 0.0, None, ALU.mult)
                v.drain()
                with v.Fori(0, BLOCKS) as b:
                    v.nop().then_inc(g_next, 1)
                    others(w)
                    V.scalar_tensor_tensor(out=piece_wgt, in0=piece_other.rearrange("p n j -> p j n"), scalar=0.0,
                                           in1=edge_values[:, bass.ds(w * PIECE, PIECE)].unsqueeze(2).broadcast_to([PS, PIECE, NB]),
                                           op0=ALU.is_equal, op1=ALU.mult).then_inc(g_wgt_ready, 1)
                    V.tensor_scalar(piece_base[:], piece_base[:], float(NB), None, ALU.add)
                    take(v, g_agg_done, 1)
                    take(v, g_sums_loaded, 16)
                    V.tensor_tensor(node_row[:, 0:F], node_row[:, 0:F], p_agg[0:NB, 0:F], ALU.add)
                    V.tensor_tensor(node_sums[:, bass.ds(b, 1)], node_sums[:, bass.ds(b, 1)], p_agg[0:NB, F:F + 1], ALU.add)
                    hand_block()
                v.nop().then_inc(g_next, 1)

            def finish(b):
                take(v, g_sums_loaded, 16)
                V.tensor_scalar(den[:, 0:1], node_sums[:, bass.ds(b, 1)], 1e-30, None, ALU.max)
                v.drain()
                V.reciprocal(den[:, 1:2], den[:, 0:1])
                v.drain()
                V.tensor_scalar(node_row[:, 0:F], node_row[:, 0:F], den[:, 1:2], None, ALU.mult)
                hand_block()
                v.nop().then_inc(g_next, 1)

            def begin():
                V.memset(node_sums[:], 0.0)
                V.memset(piece_base[:], 0.0)
                V.memset(node_row, 0.0)
                v.drain()
                v.nop().then_inc(g_next, 1)

            general_path(v, begin=begin, scores=scores_piece, maximum=maximum, weigh=weigh, clear=clear,
                         aggregate=aggregate_piece, finish=finish)

            def greatest(q, lo, hi):
                V.scalar_tensor_tensor(out=masked[:, 0:hi - lo], in0=other[:, q, lo:hi], scalar=-FAR,
                                       in1=t_edge[:, q, :].unsqueeze(1).broadcast_to([128, hi - lo, TILES]), op0=ALU.mult, op1=ALU.add)
                v.drain()
                return V.tensor_reduce(colmax[:, lo:hi], masked[:, 0:hi - lo], AX.X, ALU.max)

            def attention(i, what, q):
                b = i * 2 + q
                if what == "edges":
                    v.wait_ge(products_ready[q], i + 1)
                    V.tensor_scalar(dst_l[:], dst_t[:, q, :], block_base[:, q:q + 1], None, ALU.subtract)
                    V.tensor_reduce(s_edge[:], attr[:, q], AX.X, ALU.add)
                    v.drain()
                    wait(v, nt_done, (b - 1) * 3)
                    V.tensor_tensor(other[:, q], dst_l[:].unsqueeze(1).broadcast_to([128, NB, TILES]), node_ids[:],
                                    ALU.not_equal).then_inc(other_ready[q], 1)
                elif what == "scores0":
                    v.wait_ge(other_ready[q], i + 1)
                    v.wait_ge(gathered[q], i * (16 * TILES) + 16 * TILES)
                    V.tensor_tensor(t_edge[:, q, :], rows[:, q, :, F + 1], s_edge[:], ALU.add)
                    v.drain()
                    greatest(q, 0, NB_HALF).then_inc(half_ready, 1)
                elif what == "scores1":
                    v.wait_ge(half_ready, b + 1)
                    greatest(q, NB_HALF, NB).then_inc(colmax_ready, 1)
                elif what == "nodemax":
                    v.wait_ge(colmax_turned, b + 1)
                    V.tensor_reduce(node_t[:, 0:1], p_att[0:NB, 0:128], AX.X, ALU.max)
                    V.tensor_copy(node6[:, 0:3], sdst3[:, bass.ds(b, 1), :].rearrange("p o k -> p (o k)"))
                    v.drain()
                    V.tensor_tensor(node_t[:, 1:2], node_t[:, 0:1], sdst[:, bass.ds(b, 1)], ALU.add)
                    v.drain()
                    V.scalar_tensor_tensor(out=node_t[:, 2:3], in0=node_t[:, 1:2], scalar=ALPHA, in1=node_t[:, 1:2],
                                           op0=ALU.mult, op1=ALU.max)
                    v.drain()
                    V.tensor_copy(node6[:, 3:4], node_t[:, 2:3])
                    v.drain()
                    V.tensor_tensor(node_t[:, 3:4], node_t[:, 2:3], node6[:, 3:4], ALU.subtract)
                    v.drain()
                    V.tensor_copy(node6[:, 4:5], node_t[:, 3:4])
                    v.drain()
                    V.tensor_tensor(node6[:, 5:6], node_t[:, 3:4], node6[:, 4:5], ALU.subtract).then_inc(node_ready, 1)
                elif what == "score":
                    v.wait_ge(spread_done, b + 1)
                    V.tensor_reduce(spread[:], p_att[:, 128:128 + 6 * TILES].rearrange("p (j v k) -> p j v k", v=2, k=3),
                                    AX.X, ALU.add)
                    v.drain()
                    V.tensor_tensor(logit[:], t_edge[:, q, :], spread[:, :, 0], ALU.add)
                    v.drain()
                    V.scalar_tensor_tensor(out=score[:], in0=logit[:], scalar=ALPHA, in1=logit[:], op0=ALU.mult, op1=ALU.max)
                    v.drain()
                    V.tensor_tensor(logit[:], score[:], spread[:, :, 1], ALU.subtract)
                    v.drain()
                    V.tensor_scalar(score[:], logit[:], 0.0, None, ALU.min).then_inc(score_ready, 1)
                elif what == "weights":
                    v.wait_ge(exp_ready, b + 1)
                    wait(v, agg_turned, b)
                    V.scalar_tensor_tensor(out=wgt[:], in0=other[:, q].rearrange("p n j -> p j n"), scalar=0.0,
                                           in1=ex[:].unsqueeze(2).broadcast_to([128, TILES, NB]),
                                           op0=ALU.is_equal, op1=ALU.mult).then_inc(wgt_ready, 1)
                elif what == "den":
                    v.wait_ge(agg_done, b + 1)
                    V.tensor_scalar(den[:, 0:1], p_agg[0:NB, F:F + 1], 1e-30, None, ALU.max)
                    v.drain()
                    V.reciprocal(den[:, 1:2], den[:, 0:1]).then_inc(den_ready, 1)
                elif what == "residual":
                    v.wait_ge(projected, b + 1)
                    v.wait_ge(x_loaded[q], i * 16 + 16)
                    V.tensor_tensor(x1[:, q, :], p_mix[0:NB, F:2 * F], x1[:, q, :], ALU.add).then_inc(x1_ready, 1)
                elif what == "moments":
                    v.drain()
                    for z in range(2):
                        V.bn_stats(ln6[:, z, :], x1[:, z, :])
                    v.drain()
                    for z in range(2):
                        last = V.bn_aggr(lnmv[:, z, :], ln6[:, z, :])
                    last.then_inc(moments_ready, 1)
                elif what == "normalise":
                    v.wait_ge(lnstd_ready, i + 1)
                    wait(v, x_turned, i)
                    V.reciprocal(lnr[:], lnstd[:])
                    v.drain()
                    for z in range(2):
                        last = V.tensor_scalar(xn[:, z, :], x1[:, z, :], lnmv[:, z, 0:1], lnr[:, z:z + 1], ALU.subtract, ALU.mult)
                    last.then_inc(xn_ready, 1)
                elif what == "x_lo":
                    v.wait_ge(xT_hi_ready, i + 1)
                    V.tensor_tensor(xT[:, LO].rearrange("p c n -> p (c n)"), p_mix[:, 0:KC * 2 * NB],
                                    xT[:, HI].rearrange("p c n -> p (c n)").bitcast(F32), ALU.subtract).then_inc(xT_ready, 1)
                elif what == "route_max":
                    v.wait_ge(routed, i + 1)
                    V.tensor_reduce(r_negmax[:], p_mix[0:NB, 0:2 * EXPERTS].rearrange("p (q e) -> p q e", q=2), AX.X, ALU.max,
                                    negate=True).then_inc(negmax_ready, 1)
                elif what == "gates":
                    v.wait_ge(r_exp_ready, i + 1)
                    V.reciprocal(r_inv[:], r_sum[:])
                    v.drain()
                    for z in range(2):
                        last = V.tensor_scalar(r_w[:, z, :], r_exp[:, z, :], r_inv[:, z:z + 1], None, ALU.mult)
                    last.then_inc(r_w_ready, 1)
                elif what == "base":
                    v.wait_ge(bias_done, i + 1)
                    V.tensor_tensor(base[:], p_mix[0:NB, :].rearrange("p (q f) -> p q f", q=2), x1[:], ALU.add).then_inc(base_ready, 1)

            def experts(g, layer, e):
                n = g * EXPERTS + e
                if layer < 3:
                    h, hi_ready, ready = ((h1, h1_hi_ready, h1_ready), (h2, h2_hi_ready, h2_ready))[layer - 1]
                    v.wait_ge(hi_ready, n + 1)
                    V.tensor_tensor(h[:, e % 2, LO], h_full[:, layer - 1], h[:, e % 2, HI].bitcast(F32), ALU.subtract).then_inc(ready, 1)
                    return
                if e == 0:
                    v.wait_ge(out_stored, g * 16 + 16)
                    V.tensor_copy(gate[:], r_w[:])
                    v.drain()
                v.wait_ge(l3_done, n + 1)
                for z in range(2):
                    last = V.scalar_tensor_tensor(out=acc[:, z, :], in0=p_l3[0:NB, z * F:(z + 1) * F], scalar=gate[:, z, e:e + 1],
                                                  in1=(base if e == 0 else acc)[:, z, :], op0=ALU.mult, op1=ALU.add)
                last.then_inc(y_added, 1)

            v.wait_ge(l_small, 48)
            V.tensor_copy(wr_parts[:, HI], wr[:])
            v.drain()
            V.tensor_tensor(wr_parts[:, LO], wr[:], wr_parts[:, HI].bitcast(F32), ALU.subtract).then_inc(wr_split, 1)
            for n in range(2 * STAGED):
                v.wait_ge(last_hi_ready, n + 1)
                w = staged_weights(2 + n // STAGED, n % STAGED)
                n %= STAGED
                V.tensor_tensor(w[:, LO], w_staged[:, n], w[:, HI].bitcast(F32), ALU.subtract).then_inc(last_split, 1)
            over_groups(v, attention, experts, BEHIND["vector"], "vector" in ATTENTION_FIRST)

        @block.tensor
        def _(pe):
            T = nc.tensor
            pe.wait_ge(ident_ready, 1)
            pe.wait_ge(l_gnn, 48)
            for k in range(KC):
                for c in range(KC):
                    o = (k * KC + c) * 128
                    last = T.transpose(p_l1[:, o:o + 128], gw[:, c, k * 128:(k + 1) * 128], ident[:])
            last.then_inc(gwT_done, 1)
            for k in range(KC):
                for n in range(2):
                    for c in range(KC):
                        last = T.matmul(p_l2[:, k * 2 + n:k * 2 + n + 1], gw[:, c, k * 128:(k + 1) * 128], a_cols[:, n * KC + c:n * KC + c + 1],
                                        start=(c == 0), stop=(c == KC - 1))
            last.then_inc(u_done, 1)
            pe.wait_ge(a_wide_ready, 1)
            for n in range(2):
                for c in range(KC):
                    last = T.matmul(p_l3[:, n * F:(n + 1) * F], a_wide[:, n * KC + c, :], gw[:, c, :], start=(c == 0), stop=(c == KC - 1))
            last.then_inc(u_rows_done, 1)
            pe.wait_ge(counts_ready, 1)
            T.matmul(p_att[0:BLOCKS, 0:1], below_n, ones[0:PS, 0:1], start=True, stop=True).then_inc(counts_summed, 1)
            pe.wait_ge(gw_copied, 1)
            pe.wait_ge(u_copied, 1)
            pe.nop().then_inc(dotted, 2)
            pe.wait_ge(start_ready, 1)
            T.matmul(p_att[0:1, 120:121], falls[:], ones[0:PS, 0:1], start=True, stop=True)
            T.matmul(p_att[0:1, 64:64 + BLOCKS], start_col[:], ident[0:BLOCKS, 0:BLOCKS], start=True, stop=True).then_inc(start_turned, 1)
            pe.nop().then_inc(dots_read, 2)

            def over_chunks(c, k):
                for n, b in enumerate(ODD_BLOCKS):
                    pe.wait_ge(table_rows, c * CB + b + 1)
                    for f in range(KC):
                        last = T.transpose((p_mix, p_agg)[n][:, f * NB:(f + 1) * NB], tr[:, k, b, f * 128:(f + 1) * 128], ident[0:NB, 0:NB])
                    last.then_inc(h_turned, 1)
                pe.wait_ge(dots_read, c + 1)
                for n, b in enumerate(ODD_BLOCKS):
                    pe.wait_ge(hT_ready, c * len(ODD_BLOCKS) + n + 1)
                    for f in range(KC):
                        last = T.matmul(p_dots[k % 2][0:NB, 2 * n:2 * n + 2], hT[:, n, f * NB:(f + 1) * NB], u_cols[:, f, :],
                                        start=(f == 0), stop=(f == KC - 1))
                    last.then_inc(dotted, 1)

            with pe.Fori(0, CHUNKS // CHUNK_BUFS) as i:
                for k in range(CHUNK_BUFS):
                    over_chunks(i * CHUNK_BUFS + k, k)
            for c in range(CHUNKS // CHUNK_BUFS * CHUNK_BUFS, CHUNKS):
                over_chunks(c, c % CHUNK_BUFS)
            pe.wait_ge(bn_rows_ready, 1)
            for n in range(4):
                last = T.transpose(p_l3[:, n * R:(n + 1) * R], bn_rows[:, n, :], ident[0:R, 0:R])
            last.then_inc(bn_turned, 1)
            def turn_maxima(b):
                take(pe, g_colmax_ready, 1)
                T.transpose(p_att[0:NB, 0:128], colmax[:], ident[:]).then_inc(g_colmax_turned, 1)

            def aggregate_piece(w):
                with pe.Fori(0, BLOCKS):
                    take(pe, g_wgt_ready, 1)
                    for j in range(PIECE):
                        last = T.matmul(p_agg[0:NB, 0:F + 1], piece_wgt[:, j, :], piece_rows[:, j, 0:F + 1], start=(j == 0), stop=(j == PIECE - 1))
                    last.then_inc(g_agg_done, 1)

            pe.wait_ge(bn_cols_ready, 1)
            general_path(pe, maximum=turn_maxima, aggregate=aggregate_piece)
            pe.wait_ge(wr_split, 1)
            pe.wait_ge(l_small, 48)

            def attention(i, what, q):
                b = i * 2 + q
                if what in ("nt0", "nt1", "nt2"):
                    r = int(what[2])
                    lo, hi = NT_ROUNDS[r]
                    if r == 0:
                        pe.wait_ge(other_ready[q], i + 1)
                        wait(pe, mine_ready, b * 3)
                    if r == 2:
                        pe.wait_ge(mine_ready, b * 3 + 1)
                    for j in range(lo, hi):
                        last = T.transpose(p_nt[r % 2][0:NB, (j - lo) * 128:(j - lo + 1) * 128], other[:, q, :, j], ident_b[:])
                    last.then_inc(nt_done, 1)
                elif what == "colmax":
                    pe.wait_ge(colmax_ready, b + 1)
                    wait(pe, score_ready, b)
                    T.transpose(p_att[0:NB, 0:128], colmax[:], ident[:]).then_inc(colmax_turned, 1)
                elif what == "spread":
                    pe.wait_ge(mine_ready, b * 3 + 3)
                    pe.wait_ge(node_ready, b + 1)
                    for j in range(TILES):
                        last = T.matmul(p_att[:, 128 + 6 * j:134 + 6 * j], mine_T[:, j, :], node6[:], start=True, stop=True)
                    last.then_inc(spread_done, 1)
                elif what.startswith("aggregate"):
                    if what == "aggregate0":
                        pe.wait_ge(wgt_ready, b + 1)
                    for j in range(*AGG_PARTS[int(what[-1])]):
                        last = T.matmul(p_agg[0:NB, 0:F + 1], wgt[:, j, :], rows[:, q, j, 0:F + 1], start=(j == 0), stop=(j == TILES - 1))
                    if what == "aggregate2":
                        last.then_inc(agg_done, 1)
                elif what == "turn":
                    pe.wait_ge(agg_ready, b + 1)
                    if q == 0:
                        wait(pe, base_ready, i)
                    else:
                        pe.wait_ge(x1_ready, b)
                    for c in range(KC):
                        last = T.transpose(p_mix[:, c * NB:(c + 1) * NB], agg[:, c * 128:(c + 1) * 128], ident[0:NB, 0:NB])
                    last.then_inc(agg_turned, 1)
                elif what == "project":
                    pe.wait_ge(aggT_ready, b + 1)
                    for c in range(KC):
                        last = T.matmul(p_mix[0:NB, F:2 * F], aggT[:, c, :], gwT[:, c, :], start=(c == 0), stop=(c == KC - 1))
                    last.then_inc(projected, 1)
                elif what == "turn_x":
                    pe.wait_ge(xn_ready, i + 1)
                    pe.wait_ge(x1_ready, i * 2 + 2)
                    for c in range(KC):
                        for z in range(2):
                            o = (c * 2 + z) * NB
                            last = T.transpose(p_mix[:, o:o + NB], xn[:, z, c * 128:(c + 1) * 128], ident[0:NB, 0:NB])
                    last.then_inc(x_turned, 1)
                elif what == "route":
                    pe.wait_ge(xT_ready, i + 1)
                    for z in range(2):
                        o = p_mix[0:NB, z * EXPERTS:(z + 1) * EXPERTS]
                        for c in range(KC):
                            for x_part, w_part in PRODUCTS:
                                T.matmul(o, xT[:, x_part, c, z * NB:(z + 1) * NB], wr_parts[:, w_part, c, :],
                                         start=(c == 0 and (x_part, w_part) == PRODUCTS[0]), stop=False)
                        last = T.matmul(o, ones[0:1, 0:NB], br_row[:], start=False, stop=True)
                    last.then_inc(routed, 1)
                elif what == "turn_w":
                    pe.wait_ge(r_w_ready, i + 1)
                    for z in range(2):
                        last = T.transpose(p_mix[0:EXPERTS, z * NB:(z + 1) * NB], r_w[:, z, :], ident[0:NB, 0:NB])
                    last.then_inc(w_turned, 1)
                elif what == "bias":
                    pe.wait_ge(wT_ready, i + 1)
                    for z in range(2):
                        last = T.matmul(p_mix[0:NB, z * F:(z + 1) * F], r_wT[:, z * NB:(z + 1) * NB], bo_sb[:], start=True, stop=True)
                    last.then_inc(bias_done, 1)

            def experts(g, layer, e):
                n = g * EXPERTS + e
                if layer == 1:
                    if e == 0:
                        pe.wait_ge(xT_ready, g + 1)
                        pe.wait_ge(w_split, 2 * STAGED)
                        pe.wait_ge(last_split, 2 * STAGED)
                    pe.wait_ge(h1_ready, n + 1)
                    for m in range(KC):
                        for c in range(KC):
                            for a, b in PRODUCTS:
                                last = T.matmul(p_l1[:, m * 2 * NB:(m + 1) * 2 * NB], w1[:, a, e * KC + c, m * 128:(m + 1) * 128], xT[:, b, c, :],
                                                start=(c == 0 and (a, b) == PRODUCTS[0]), stop=(c == KC - 1 and (a, b) == PRODUCTS[-1]))
                    last.then_inc(l1_done, 1)
                elif layer == 2:
                    pe.wait_ge(h2_ready, n + 1)
                    pe.wait_ge(h1_ready, n + 2)
                    for m in range(KC):
                        for c in range(KC):
                            for a, b in PRODUCTS:
                                last = T.matmul(p_l2[:, m * 2 * NB:(m + 1) * 2 * NB], w2[:, a, e * KC + c, m * 128:(m + 1) * 128], h1[:, e % 2, b, c, :],
                                                start=(c == 0 and (a, b) == PRODUCTS[0]), stop=(c == KC - 1 and (a, b) == PRODUCTS[-1]))
                    last.then_inc(l2_done, 1)
                else:
                    pe.wait_ge(y_added, n + 1)
                    pe.wait_ge(h2_ready, n + 2)
                    for z in range(2):
                        for c in range(KC):
                            for a, b in PRODUCTS:
                                last = T.matmul(p_l3[0:NB, z * F:(z + 1) * F], h2[:, e % 2, a, c, z * NB:(z + 1) * NB], wo[:, b, e * KC + c, :],
                                                start=(c == 0 and (a, b) == PRODUCTS[0]), stop=(c == KC - 1 and (a, b) == PRODUCTS[-1]))
                    last.then_inc(l3_done, 1)

            over_groups(pe, attention, experts, 0, "tensor" in ATTENTION_FIRST)


_INS = ['x', 'src', 'dst', 'edge_attr_64', 'L0_gnn_W', 'L0_gnn_A', 'L0_ffn_Wr', 'L0_ffn_br', 'L0_ffn_W1', 'L0_ffn_b1',
        'L0_ffn_g1', 'L0_ffn_be1', 'L0_ffn_m1', 'L0_ffn_v1', 'L0_ffn_W2', 'L0_ffn_b2', 'L0_ffn_g2', 'L0_ffn_be2',
        'L0_ffn_m2', 'L0_ffn_v2', 'L0_ffn_Wo', 'L0_ffn_bo']


def kernel(**inputs):
    import numpy as _np
    import concourse.bacc as _bacc
    from concourse.bass_utils import run_bass_kernel_spmd as _run

    nc = _bacc.Bacc("TRN2", target_bir_lowering=False, num_devices=1)
    arrays, args = {}, []
    for name in _INS:
        a = _np.ascontiguousarray(inputs[name])
        arrays[f"in_{name}_dram"] = a
        args.append(nc.dram_tensor(f"in_{name}_dram", a.shape, mybir.dt.from_np(a.dtype), kind="ExternalInput").ap())
    out = nc.dram_tensor("out_dram", (NODES, F), F32, kind="ExternalOutput").ap()
    gnn_ffn_program(nc, *args, out)
    r = _run(nc, [arrays], core_ids=[0])
    return _np.asarray(r.results[0]["out_dram"])
```
